# Optimizing a Trainium2 kernel written in Bass

```python
import numpy as np
import jax
import jax.numpy as jnp

def _softmax(x, axis=-1):
    return jax.nn.softmax(x, axis=axis)

def _gelu(x):
    return jax.nn.gelu(x, approximate=True)

def _silu(x):
    return jax.nn.silu(x)

def _sigmoid(x):
    return jax.nn.sigmoid(x)

def _layernorm(x, axis=-1, eps=1e-05):
    m = jnp.mean(x, axis=axis, keepdims=True)
    v = jnp.var(x, axis=axis, keepdims=True)
    return (x - m) / jnp.sqrt(v + eps)

def _scatter_add(tgt, idx, src, axis=0):
    return tgt.at[idx].add(src)

def _segment_sum(src, seg, n):
    return jax.ops.segment_sum(src, seg, n)
kernel_name = 'mk_adj_preln_d2_adj_r2_a414c7'

def setup_inputs(seed: int=0):
    np.random.seed(seed)
    _w = jnp.asarray

    def _rec_inputs():
        import jax
        import jax.numpy as jnp
        _gk = jax.random.key(seed)
        x = -0.0004039 + 1 * jax.random.normal(jax.random.fold_in(_gk, 1), (32, 256, 384), jnp.float32)
        _w = (1.0 + jnp.arange(256, dtype=jnp.float32)) ** (-0.5)
        _w = _w / _w.mean()
        _pij = jnp.clip(0.03125 * _w[:, None] * _w[None, :], 0.0, 1.0)
        _a = jax.random.uniform(jax.random.fold_in(_gk, 2), (32, 256, 256)) < _pij
        _af = _a.astype(jnp.float32)
        adj = _af
        return (x, adj)
    x, adj = _rec_inputs()

    def _L0_gnn_setup():
        import jax, jax.numpy as jnp
        import numpy as np
        B, S, H, L = (32, 256, 384, 2)

        def _layer_norm(z, a, b, eps=0.001):
            mu = jnp.mean(z, axis=-1, keepdims=True)
            sigma = jnp.std(z, axis=-1, keepdims=True, ddof=1)
            return (z - mu) / (sigma + eps) * a + b
        key = jax.random.key(seed)
        ks = jax.random.split(key, 6)
        hidden_state = jax.random.normal(ks[0], (B, S, H), dtype=jnp.float32)
        adjacency_matrix = (jax.random.uniform(ks[1], (B, S, S)) < 0.2).astype(jnp.float32)
        W_left = 0.05 * jax.random.normal(ks[2], (L, H, H), dtype=jnp.float32)
        W_right = 0.05 * jax.random.normal(ks[3], (L, H, H), dtype=jnp.float32)
        W_lin = 0.05 * jax.random.normal(ks[4], (L, H, H), dtype=jnp.float32)
        b_lin = jnp.zeros((L, H), dtype=jnp.float32)
        ln_a = jnp.ones((L, H), dtype=jnp.float32)
        ln_b = jnp.zeros((L, H), dtype=jnp.float32)
        return {'hidden_state': hidden_state, 'adjacency_matrix': adjacency_matrix, 'W_left': W_left, 'W_right': W_right, 'W_lin': W_lin, 'b_lin': b_lin, 'ln_a': ln_a, 'ln_b': ln_b}
    _L0_gnn_all = _L0_gnn_setup()
    _L0_gnn_in = {k: v for k, v in _L0_gnn_all.items() if k in ('W_left', 'W_right', 'W_lin', 'b_lin', 'ln_a', 'ln_b')}
    del _L0_gnn_all

    def _L1_gnn_setup():
        import jax, jax.numpy as jnp
        import numpy as np
        NUM_HEADS = 12
        HIDDEN = 384
        HEAD = HIDDEN // NUM_HEADS
        B, N = (16, 256)
        key = jax.random.key(seed)
        ks = jax.random.split(key, 9)
        s = 0.02
        return {'x': jax.random.normal(ks[0], (B, N, HIDDEN), jnp.float32), 'spatial_encoding': jax.random.normal(ks[1], (B, N, N), jnp.float32), 'edge_encoding': jax.random.normal(ks[2], (B, N, N), jnp.float32), 'Wq': jax.random.normal(ks[3], (HIDDEN, HIDDEN), jnp.float32) * s, 'Wk': jax.random.normal(ks[4], (HIDDEN, HIDDEN), jnp.float32) * s, 'Wv': jax.random.normal(ks[5], (HIDDEN, HIDDEN), jnp.float32) * s, 'bv': jax.random.normal(ks[6], (HIDDEN,), jnp.float32) * s, 'Wo': jax.random.normal(ks[7], (HIDDEN, HIDDEN), jnp.float32) * s, 'bo': jax.random.normal(ks[8], (HIDDEN,), jnp.float32) * s}
    _L1_gnn_all = _L1_gnn_setup()
    _L1_gnn_in = {k: v for k, v in _L1_gnn_all.items() if k in ('Wq', 'Wk', 'Wv', 'bv', 'Wo', 'bo')}
    del _L1_gnn_all
    return {'x': x, 'adj': adj, 'L0_gnn_W_left': _L0_gnn_in['W_left'], 'L0_gnn_W_right': _L0_gnn_in['W_right'], 'L0_gnn_W_lin': _L0_gnn_in['W_lin'], 'L0_gnn_b_lin': _L0_gnn_in['b_lin'], 'L0_gnn_ln_a': _L0_gnn_in['ln_a'], 'L0_gnn_ln_b': _L0_gnn_in['ln_b'], 'L1_gnn_Wq': _L1_gnn_in['Wq'], 'L1_gnn_Wk': _L1_gnn_in['Wk'], 'L1_gnn_Wv': _L1_gnn_in['Wv'], 'L1_gnn_bv': _L1_gnn_in['bv'], 'L1_gnn_Wo': _L1_gnn_in['Wo'], 'L1_gnn_bo': _L1_gnn_in['bo']}

def reference(x, adj, L0_gnn_W_left, L0_gnn_W_right, L0_gnn_W_lin, L0_gnn_b_lin, L0_gnn_ln_a, L0_gnn_ln_b, L1_gnn_Wq, L1_gnn_Wk, L1_gnn_Wv, L1_gnn_bv, L1_gnn_Wo, L1_gnn_bo):
    import jax
    import jax.numpy as jnp

    def _L0_gnn_ref(hidden_state, adjacency_matrix, W_left, W_right, W_lin, b_lin, ln_a, ln_b):
        import jax, jax.numpy as jnp
        import numpy as np
        B, S, H, L = (32, 256, 384, 2)

        def _layer_norm(z, a, b, eps=0.001):
            mu = jnp.mean(z, axis=-1, keepdims=True)
            sigma = jnp.std(z, axis=-1, keepdims=True, ddof=1)
            return (z - mu) / (sigma + eps) * a + b
        temper = float(np.sqrt(H))
        adj = adjacency_matrix
        adj_tri = jnp.triu(adj, k=1)
        diag_mask = jnp.triu(adj, k=0) - adj_tri
        h = hidden_state
        for l in range(L):
            m_left = jnp.einsum('bsh,oh->bso', h, W_left[l])
            m_right = jnp.einsum('bsh,oh->bso', h, W_right[l])
            u_left = jnp.einsum('bih,bjh->bij', h, m_left) / temper
            u_right = jnp.einsum('bih,bjh->bij', h, m_right) / temper
            u = u_left * adj_tri + u_left * diag_mask + u_right * jnp.swapaxes(adj_tri, 1, 2)
            delta_exp_u = jnp.exp(u) * adj
            attention = delta_exp_u / (jnp.sum(delta_exp_u, axis=2, keepdims=True) + 1e-10)
            h_lin = jnp.einsum('bsh,oh->bso', h, W_lin[l]) + b_lin[l]
            ctx = jnp.matmul(attention, h_lin)
            h = jax.nn.relu(_layer_norm(ctx, ln_a[l], ln_b[l]))
        return h

    def _L1_gnn_ref(x, spatial_encoding, edge_encoding, Wq, Wk, Wv, bv, Wo, bo):
        import jax, jax.numpy as jnp
        import numpy as np
        NUM_HEADS = 12
        HIDDEN = 384
        HEAD = HIDDEN // NUM_HEADS
        B, N = (16, 256)
        b, n, h = x.shape
        scale = jnp.asarray(HIDDEN, x.dtype) ** (-0.5)
        q = (x @ Wq.T).reshape(b, n, NUM_HEADS, HEAD)
        k = (x @ Wk.T).reshape(b, n, NUM_HEADS, HEAD)
        v = (x @ Wv.T + bv).reshape(b, n, NUM_HEADS, HEAD)
        bias = (spatial_encoding + edge_encoding)[:, None]
        scores = jnp.einsum('bqhd,bkhd->bhqk', q, k) * scale + bias
        row_nonzero = jnp.any(scores != 0, axis=-1, keepdims=True)
        scores = jnp.where(row_nonzero, scores, -jnp.inf)
        p = jax.nn.softmax(scores, axis=-1)
        p = jnp.nan_to_num(p)
        out = jnp.einsum('bhqk,bkhd->bqhd', p, v).reshape(b, n, h)
        return out @ Wo.T + bo
    h = jnp.maximum(_layernorm(x, axis=-1), 0.0)
    x = x + _L0_gnn_ref(h, adj, L0_gnn_W_left, L0_gnn_W_right, L0_gnn_W_lin, L0_gnn_b_lin, L0_gnn_ln_a, L0_gnn_ln_b)
    h = jnp.maximum(_layernorm(x, axis=-1), 0.0)
    x = x + _L1_gnn_ref(h, adj, adj, L1_gnn_Wq, L1_gnn_Wk, L1_gnn_Wv, L1_gnn_bv, L1_gnn_Wo, L1_gnn_bo)
    return x

_drawn_inputs = setup_inputs


def setup_inputs(seed=0):
    import zlib

    import numpy as np

    out = dict(_drawn_inputs(seed))
    spreads = {'L0_gnn_b_lin': (0.0, 0.1), 'L0_gnn_ln_a': (1.0, 0.2), 'L0_gnn_ln_b': (0.0, 0.1)}
    factors = {'L0_gnn_W_right': 4.795,
     'L1_gnn_Wq': 61.692,
     'L1_gnn_Wk': 61.998,
     'L1_gnn_bv': 7.941,
     'L1_gnn_bo': 3.776}
    for name, (base, spread) in spreads.items():
        noise = np.random.default_rng([zlib.crc32(name.encode()), seed]).standard_normal(out[name].shape)
        drawn = base * np.exp(spread * noise) if base else spread * noise
        out[name] = jnp.asarray(drawn.astype(out[name].dtype))
    for name, factor in factors.items():
        out[name] = (out[name] * factor).astype(out[name].dtype)
    return out
```

```python
from contextlib import ExitStack

import concourse.bass as bass
from concourse import mybir

F32 = mybir.dt.float32
F32R = mybir.dt.float32r
ALU = mybir.AluOpType
ACT = mybir.ActivationFunctionType
AX = mybir.AxisListType

P = 128
GRAPHS, NODES, H = 32, 256, 384
LAYERS, HEADS = 2, 12
D = H // HEADS
KC = H // P
NB = NODES // P
HPC = P // D
PAIRS = HEADS * NB // 2
PPC = PAIRS // KC

EPS_PRE = 1e-5
EPS_STD = 1e-3
EPS_SUM = 1e-10
BIG = 3.4e38

TILE = {"T": 0, "G": NB, "H": NB + KC, "U": 2 * NB + KC, "X": 3 * NB + KC}
LAYER_TILES = 4 * NB + KC
GNN_TILES = LAYERS * LAYER_TILES
GNN_BANKS = 3
SPLITS = NB + KC
PROJ = {("CT", 0): 0, ("CT", 1): 1, ("QK", 0): 2, ("QK", 1): 3, ("V", 0): 4, ("V", 1): 5, ("QK", 2): 6,
        ("O", 0): 7, ("O", 1): 8, ("O", 2): 9, ("Y", 0): 10, ("Y", 1): 11}
PROJ_TILES = len(PROJ)
PROJ_SPLIT = {("CT", 0): 0, ("CT", 1): 1, ("QK", 0): 2, ("QK", 1): 3, ("QK", 2): 4}
GNN_W = ["left0", "right0", "lin0", "left1", "right1", "lin1"]
WEIGHTS = GNN_W + ["q", "k", "v", "o"]
FIRST_WEIGHTS = 3
SPREAD_DMAS = 2 * P // D


def attention_step(k):
    return ([("S", k)] if k < PAIRS else []) + ([("P", k - 1)] if k else []) + ([("EX", k)] if k < PAIRS else [])


ORDER = (
    [("CLN",), ("T", 0), ("G", 0, 0), ("CNORM",), ("G", 0, 1), ("CT",), ("G", 0, 2), ("QK", 0), ("H", 0, 0),
     ("QK", 1), ("H", 0, 1), ("U", 0, 0), ("E", 0, 0), ("U", 0, 1), ("E", 0, 1), ("V", 0)]
    + attention_step(0) + [("V", 1)] + attention_step(1)
    + [("X", 0, 0), ("X", 0, 1), ("XN", 0, 0), ("QK", 2), ("XN", 0, 1)]
    + attention_step(2) + attention_step(3) + [("T", 1), ("G", 1, 0)]
    + attention_step(4) + [("G", 1, 1), ("R", 0), ("O", 0)]
    + attention_step(5) + [("G", 1, 2)]
    + attention_step(6) + [("H", 1, 0)]
    + attention_step(7) + [("H", 1, 1)]
    + attention_step(8) + [("R", 1), ("O", 1), ("U", 1, 0), ("E", 1, 0)]
    + attention_step(9) + [("U", 1, 1), ("E", 1, 1), ("LNX",)]
    + attention_step(10) + attention_step(11)
    + [("X", 1, 0), ("X", 1, 1), ("XN", 1, 0), ("XN", 1, 1)]
    + attention_step(12) + [("R", 2), ("O", 2), ("Y", 0), ("Y", 1)]
)
GNN_STEPS = {"T", "G", "H", "U", "E", "X", "XN"}
NEXT_STEPS = {"LNX"}


def steps_of(gnn, attention, following):
    for s in ORDER:
        if s[0] in GNN_STEPS:
            if gnn:
                yield s
        elif s[0] in NEXT_STEPS:
            if following:
                yield s
        elif attention:
            yield s


def build(nc, x, adj, adj_t, w, vec, out):
    ctx = ExitStack()
    with ctx:
        def sb(name, shape, dt=F32):
            return ctx.enter_context(nc.sbuf_tensor(name, shape, dt))

        def bank(name):
            return ctx.enter_context(nc.psum_tensor(name, [P, 512], F32))

        passed = ctx.enter_context(nc.semaphore("passed"))

        class Count:

            def __init__(self, name, per, first=0, unit=1):
                self.sem = ctx.enter_context(nc.semaphore(name))
                self.per, self.first, self.unit = per, first, unit

            def at(self, n, k):
                return n * (self.per * self.unit) + (k - self.first * self.per) * self.unit

            def due(self, n, k):
                value = self.at(n, k)
                return not isinstance(value, int) or value > 0

        w_hi = {k: sb(f"w_hi_{k}", [P, KC, H], F32R) for k in WEIGHTS}
        w_lo = {k: sb(f"w_lo_{k}", [P, KC, H], F32R) for k in WEIGHTS}
        ln_a = [sb(f"ln_a{l}", [P, H]) for l in range(LAYERS)]
        ln_b = [sb(f"ln_b{l}", [P, H]) for l in range(LAYERS)]
        b_lin = [sb(f"b_lin{l}", [P, H]) for l in range(LAYERS)]
        b_v = sb("b_v", [P, H])
        b_o = sb("b_o", [P, H])
        ident = sb("ident", [P, P])
        power = sb("power", [P, 2, NB])
        x_in = sb("x_in", [P, NB, H])
        x_res = sb("x_res", [P, NB, H])
        adj_n = sb("adj_n", [P, NB, NODES])
        adj_tr = sb("adj_tr", [P, NB, NODES])
        mask = sb("mask", [P, NB, 3 * P])
        hT_hi = sb("hT_hi", [P, KC, NODES], F32R)
        hT_lo = sb("hT_lo", [P, KC, NODES], F32R)
        g_hi = sb("g_hi", [P, KC, 2 * NODES], F32R)
        g_lo = sb("g_lo", [P, KC, 2 * NODES], F32R)
        h_lin = sb("h_lin", [P, NB, H + 2])
        att = sb("att", [P, NB, 3 * P])
        z = sb("z", [P, NB, H])
        x1 = sb("x1", [P, NB, H])
        stats = sb("stats", [P, NB, 6])
        mean_var = sb("mean_var", [P, NB, 2])
        std = sb("std", [P, NB])
        eps_sum = sb("eps_sum", [P, NB])
        rstd = sb("rstd", [P, NB])
        x_stats = sb("x_stats", [P, NB, 6])
        x_mv = sb("x_mv", [P, NB, 2])
        x_var = sb("x_var", [P, NB])
        x_rstd = sb("x_rstd", [P, NB])
        adj_c = sb("adj_c", [P, NB, NODES])
        c_stats = sb("c_stats", [P, NB, 6])
        c_mv = sb("c_mv", [P, NB, 2])
        c_var = sb("c_var", [P, NB])
        c_rstd = sb("c_rstd", [P, NB])
        acc = sb("acc", [P, NB, H])
        cT_hi = sb("cT_hi", [P, KC, NODES], F32R)
        cT_lo = sb("cT_lo", [P, KC, NODES], F32R)
        qk_hi = sb("qk_hi", [P, 2, NODES], F32R)
        qk_lo = sb("qk_lo", [P, 2, NODES], F32R)
        q_stack = sb("q_stack", [P, 2, HPC, NODES], F32R)
        k_stack = sb("k_stack", [P, 2, HPC, NODES], F32R)
        v = sb("v", [P, NB, H])
        neg_t = sb("neg_t", [P, 2, 2, NODES])
        neg_max = sb("neg_max", [P, 2 * PAIRS])
        any_t = sb("any_t", [P, 2 * PAIRS])
        row_sum = sb("row_sum", [P, 2 * PAIRS])
        inv_sum = sb("inv_sum", [P, 2 * PAIRS])
        row_scale = sb("row_scale", [P, 2 * PAIRS])
        prob = sb("prob", [P, 2, 2, NODES])
        prob_t = sb("prob_t", [P, NB, HPC, NODES])
        c_norm = prob_t[:, 0, 0:3, :].rearrange("p a b -> p (a b)").rearrange("p (s h) -> p s h", s=NB)
        scale_t = sb("scale_t", [P, NODES])
        o_raw = sb("o_raw", [P, NODES])
        oT_hi = sb("oT_hi", [P, KC, NODES], F32R)
        oT_lo = sb("oT_lo", [P, KC, NODES], F32R)

        gnn_bank = [bank(f"gnn_bank{i}") for i in range(GNN_BANKS)]
        proj_bank = [bank(f"proj_bank{i}") for i in range(2)]
        score_bank = [bank(f"score_bank{i}") for i in range(2)]
        pT_bank = bank("pT_bank")

        vec_loaded = Count("vec_loaded", 0)
        pieces = [(k, c) for k in WEIGHTS for c in range(KC)]
        stages = [prob_t[:, :, :, :].rearrange("p a b c -> p (a b c)")[:, i * H:(i + 1) * H] for i in range(5)]
        piece_loaded = [ctx.enter_context(nc.semaphore(f"piece_loaded{i}")) for i in range(len(stages))]
        piece_hi = ctx.enter_context(nc.semaphore("piece_hi"))
        piece_lo = ctx.enter_context(nc.semaphore("piece_lo"))
        consts = ctx.enter_context(nc.semaphore("consts"))
        x_loaded = Count("x_loaded", 1, unit=16)
        xres_loaded = Count("xres_loaded", 1, unit=16)
        adjn_loaded = Count("adjn_loaded", 1, unit=16)
        adjt_loaded = Count("adjt_loaded", 1, unit=16)
        adjc_loaded = Count("adjc_loaded", 1, first=1, unit=16)
        out_stored = Count("out_stored", 1, first=1, unit=16)
        x_chain = Count("x_chain", 5)
        x_rstd_ready = Count("x_rstd_ready", 1)
        x_normed = Count("x_normed", NB)
        mask_ready = Count("mask_ready", 1)
        mask_part = Count("mask_part", 3 * NB)
        gnn_full = Count("gnn_full", GNN_TILES)
        gnn_free = Count("gnn_free", GNN_TILES)
        gnn_hi = Count("gnn_hi", LAYERS * SPLITS)
        u_masked = Count("u_masked", LAYERS * NB)
        u_exp = Count("u_exp", LAYERS * NB)
        att_ready = Count("att_ready", LAYERS * NB)
        z_stats = Count("z_stats", 2 * LAYERS * NB)
        z_std = Count("z_std", LAYERS * NB)
        z_eps = Count("z_eps", LAYERS * NB)
        z_den = Count("z_den", LAYERS * NB)
        z_inv = Count("z_inv", LAYERS * NB)
        z_part = Count("z_part", NB)
        h_next = Count("h_next", LAYERS * NB)
        c_chain = Count("c_chain", 5, first=1)
        c_rstd_ready = Count("c_rstd_ready", 1, first=1)
        c_normed = Count("c_normed", NB, first=1)
        acc_ready = Count("acc_ready", NB, first=1)
        proj_full = Count("proj_full", PROJ_TILES, first=1)
        proj_free = Count("proj_free", PROJ_TILES, first=1)
        proj_hi = Count("proj_hi", len(PROJ_SPLIT), first=1)
        spread = [Count("spread0", 2 * SPREAD_DMAS, first=1, unit=16), Count("spread1", SPREAD_DMAS, first=1, unit=16)]
        score_full = Count("score_full", PAIRS, first=1)
        score_free = Count("score_free", PAIRS, first=1)
        any_ready = Count("any_ready", PAIRS, first=1)
        prob_ready = Count("prob_ready", PAIRS, first=1)
        pT_full = Count("pT_full", PAIRS, first=1)
        pT_free = Count("pT_free", PAIRS, first=1)
        inv_ready = Count("inv_ready", KC, first=1)
        scale_ready = Count("scale_ready", KC, first=1)
        scale_spread = Count("scale_spread", KC, first=1)
        o_part = Count("o_part", KC, first=1)
        o_split = Count("o_split", KC, first=1)

        def gnn_tile(kind, l, i):
            t = l * LAYER_TILES + TILE[kind] + i
            return t, gnn_bank[t % GNN_BANKS]

        def gnn_before(t):
            if t >= GNN_BANKS:
                return t - GNN_BANKS
            return max(u for u in range(GNN_TILES) if u % GNN_BANKS == t) - GNN_TILES

        def proj_tile(*key):
            t = PROJ[key]
            return t, proj_bank[t % 2]

        def node_cols(s):
            return slice((NB - 1 - s) * P, (NB - s) * P)

        def vec_loaded_all(eng):
            eng.wait_ge(vec_loaded.sem, 16 * 8)

        block = ctx.enter_context(nc.Block())

        @block.sync
        def _(sp):
            def load_piece(i):
                if i >= len(stages):
                    sp.wait_ge(piece_lo, i - len(stages) + 1)
                k, c = pieces[i]
                sp.dma_start(stages[i % len(stages)], w[WEIGHTS.index(k), c * P:(c + 1) * P, :])\
                    .then_inc(piece_loaded[i % len(stages)], 16)

            def load_x(n):
                sp.dma_start(x_in[:, :, :], x[n].rearrange("(s p) h -> p s h", p=P)).then_inc(x_loaded.sem, 16)

            def load_graph(n):
                if mask_ready.due(n, 0):
                    sp.wait_ge(mask_ready.sem, mask_ready.at(n, 0))
                    sp.sem_inc(passed, 1)
                sp.dma_start(adj_n[:, :, :], adj[n].rearrange("(s p) j -> p s j", p=P)).then_inc(adjn_loaded.sem, 16)
                if att_ready.due(n, 0):
                    sp.wait_ge(att_ready.sem, att_ready.at(n, 0))
                    sp.sem_inc(passed, 1)
                sp.dma_start(adj_tr[:, :, :], adj_t[n].rearrange("s p j -> p s j")).then_inc(adjt_loaded.sem, 16)
                if h_next.due(n, 0):
                    sp.wait_ge(h_next.sem, h_next.at(n, 0))
                    sp.sem_inc(passed, 1)
                sp.dma_start(x_res[:, :, :], x[n].rearrange("(s p) h -> p s h", p=P)).then_inc(xres_loaded.sem, 16)

            def stack_parts(n, c):
                sp.wait_ge(proj_free.sem, proj_free.at(n, PROJ["QK", c] + 1))
                sp.sem_inc(passed, 1)
                if score_full.due(n, (PAIRS - PAIRS, 2 * PPC - PAIRS, PPC)[c]):
                    sp.wait_ge(score_full.sem, score_full.at(n, (PAIRS - PAIRS, 2 * PPC - PAIRS, PPC)[c]))
                    sp.sem_inc(passed, 1)
                for d in range(P // D):
                    for i, (stack, part) in enumerate(((q_stack, (qk_hi, qk_lo)[d % 2]),
                                                       (k_stack, (qk_hi, qk_lo)[d // 2]))):
                        sp.dma_start(stack[d * D:(d + 1) * D, c % 2, :, :].bitcast(F32), part[:, i, :].bitcast(F32))\
                            .then_inc(spread[c % 2].sem, 16)

            def iteration(n, gnn, attention, following):
                if attention:
                    if score_free.due(n, 0):
                        sp.wait_ge(score_free.sem, score_free.at(n, 0))
                        sp.sem_inc(passed, 1)
                    sp.dma_start(adj_c[:, :, :], adj[n - 1].rearrange("(s p) j -> p s j", p=P))\
                        .then_inc(adjc_loaded.sem, 16)
                if gnn:
                    load_graph(n)
                if following:
                    sp.wait_ge(gnn_full.sem, gnn_full.at(n, NB))
                    sp.sem_inc(passed, 1)
                    load_x(n + 1)
                if attention:
                    for c in range(KC):
                        stack_parts(n, c)
                    sp.wait_ge(proj_free.sem, proj_free.at(n, PROJ_TILES))
                    sp.sem_inc(passed, 1)
                    sp.dma_start(out[n - 1].rearrange("(s p) h -> p s h", p=P), acc[:, :, :])\
                        .then_inc(out_stored.sem, 16)

            load_x(0)
            for i in range(len(stages)):
                load_piece(i)
            for i, t in enumerate([b_lin[0], b_lin[1], ln_a[0], ln_a[1], ln_b[0], ln_b[1], b_v, b_o]):
                sp.dma_start(t[:, :], vec[i:i + 1, :].to_broadcast([P, H])).then_inc(vec_loaded.sem, 16)
            for i in range(len(stages), FIRST_WEIGHTS * KC):
                load_piece(i)
            load_graph(0)
            for i in range(FIRST_WEIGHTS * KC, len(pieces)):
                load_piece(i)
            sp.wait_ge(gnn_full.sem, gnn_full.at(0, NB))
            sp.sem_inc(passed, 1)
            load_x(1)
            iteration(1, True, True, True)
            with sp.Fori(2, GRAPHS - 1) as n:
                iteration(n, True, True, True)
            iteration(GRAPHS - 1, True, True, False)
            iteration(GRAPHS, False, True, False)
            sp.wait_ge(out_stored.sem, out_stored.at(GRAPHS, 1))
            sp.sem_inc(passed, 1)

        @block.gpsimd
        def _(pool):
            def build_masks(n):
                pool.wait_ge(adjn_loaded.sem, adjn_loaded.at(n, 1))
                pool.sem_inc(passed, 1)
                pool.wait_ge(adjt_loaded.sem, adjt_loaded.at(n, 1))
                pool.sem_inc(passed, 1)
                if gnn_free.due(n, TILE["U"] + NB + LAYER_TILES - GNN_TILES):
                    pool.wait_ge(gnn_free.sem, gnn_free.at(n, TILE["U"] + NB + LAYER_TILES - GNN_TILES))
                    pool.sem_inc(passed, 1)
                for b in range(NB):
                    pool.affine_select(out=mask[:, b, 0:P], in_=adj_tr[:, b, 0:P], compare_op=ALU.is_ge, fill=0.0,
                                       base=0, pattern=[[-1, P]], channel_multiplier=1).then_inc(mask_part.sem, 1)
                    src = adj_n[:, 0, P:2 * P] if b == 0 else adj_tr[:, 1, P:2 * P]
                    pool.tensor_scalar(mask[:, b, P:2 * P], src, 1.0, 0.0, ALU.mult, ALU.add)\
                        .then_inc(mask_part.sem, 1)
                    last = pool.affine_select(out=mask[:, b, 2 * P:3 * P], in_=adj_n[:, b, b * P:(b + 1) * P],
                                              compare_op=ALU.is_ge, fill=0.0, base=-1, pattern=[[1, P]],
                                              channel_multiplier=-1)
                    if b < NB - 1:
                        last.then_inc(mask_part.sem, 1)
                last.then_inc(mask_ready.sem, 1)

            def iteration(n, gnn, attention, following):
                for step in steps_of(gnn, attention, following):
                    kind = step[0]
                    if kind == "CLN":
                        pool.wait_ge(c_chain.sem, c_chain.at(n, 5))
                        pool.tensor_tensor(c_rstd[:, :], c_var[:, :], power[:, 1, :], ALU.pow)\
                            .then_inc(c_rstd_ready.sem, 1)
                        if out_stored.due(n, 0):
                            pool.wait_ge(out_stored.sem, out_stored.at(n, 0))
                        for s in range(NB):
                            pool.tensor_tensor(acc[:, s, :], x1[:, s, :], b_o[:, :], ALU.add)\
                                .then_inc(acc_ready.sem, 1)
                    elif kind == "T" and step[1] == 0:
                        build_masks(n)
                    elif kind == "E":
                        _, l, j = step
                        pool.wait_ge(u_exp.sem, u_exp.at(n, NB * l + j + 1))
                        pool.tensor_tensor(att[:, j, 0:NODES], att[:, j, 0:NODES], adj_tr[:, j, :], ALU.mult)\
                            .then_inc(att_ready.sem, 1)
                    elif kind == "X":
                        _, l, s = step
                        pool.wait_ge(z_stats.sem, z_stats.at(n, 2 * (NB * l + s) + 2))
                        pool.tensor_tensor(std[:, s:s + 1], mean_var[:, s, 1:2], power[:, 0, 0:1], ALU.pow)\
                            .then_inc(z_std.sem, 1)
                    elif kind == "LNX":
                        ln_x(n + 1)

            def ln_x(n):
                pool.wait_ge(x_chain.sem, x_chain.at(n, 5))
                pool.tensor_tensor(x_rstd[:, :], x_var[:, :], power[:, 1, :], ALU.pow).then_inc(x_rstd_ready.sem, 1)

            pool.memset(power[:, 0, :], 0.5).then_inc(consts, 1)
            pool.memset(power[:, 1, :], -0.5).then_inc(consts, 1)
            pool.memset(h_lin[:, :, H:H + 2], 1.0).then_inc(consts, 1)
            pool.memset(ident[:, :], 0.0).then_inc(consts, 1)
            pool.wait_ge(consts, 4)
            pool.affine_select(out=ident[:, :], in_=ident[:, :], compare_op=ALU.not_equal, fill=1.0, base=0,
                               pattern=[[-1, P]], channel_multiplier=1).then_inc(consts, 1)
            vec_loaded_all(pool)
            ln_x(0)
            iteration(0, True, False, True)
            iteration(1, True, True, True)
            with pool.Fori(2, GRAPHS - 1) as n:
                iteration(n, True, True, True)
            iteration(GRAPHS - 1, True, True, False)
            iteration(GRAPHS, False, True, False)

        @block.scalar
        def _(act):
            def split_piece(i):
                k, c = pieces[i]
                act.wait_ge(piece_loaded[i % len(stages)], 16 * (i // len(stages) + 1))
                act.activation(w_hi[k][:, c, :], stages[i % len(stages)], ACT.Copy).then_inc(piece_hi, 1)

            def transposed_hi(n, l, s):
                t, tile = gnn_tile("T", l, s)
                act.wait_ge(gnn_full.sem, gnn_full.at(n, t + 1))
                act.activation(hT_hi[:, :, node_cols(s)], tile[:, 0:H].rearrange("p (c m) -> p c m", c=KC), ACT.Relu)\
                    .then_inc(gnn_hi.sem, 1)

            def iteration(n, gnn, attention, following):
                for step in steps_of(gnn, attention, following):
                    if later_pieces:
                        split_piece(later_pieces.pop(0))
                    kind = step[0]
                    if kind == "T":
                        for s in range(NB):
                            transposed_hi(n, step[1], s)
                    elif kind == "G":
                        _, l, c = step
                        t, tile = gnn_tile("G", l, c)
                        act.wait_ge(gnn_full.sem, gnn_full.at(n, t + 1))
                        act.activation(g_hi[:, c, :], tile[:, :], ACT.Copy).then_inc(gnn_hi.sem, 1)
                    elif kind == "E":
                        _, l, j = step
                        act.wait_ge(u_masked.sem, u_masked.at(n, NB * l + j + 1))
                        act.activation(att[:, j, 0:NODES], att[:, j, 0:NODES], ACT.Exp, scale=float(H) ** -0.5)\
                            .then_inc(u_exp.sem, 1)
                    elif kind == "CT":
                        for s in range(NB):
                            t, tile = proj_tile("CT", s)
                            act.wait_ge(proj_full.sem, proj_full.at(n, t + 1))
                            act.activation(cT_hi[:, :, s * P:(s + 1) * P],
                                           tile[:, 0:H].rearrange("p (c m) -> p c m", c=KC), ACT.Relu)\
                                .then_inc(proj_hi.sem, 1)
                    elif kind == "QK":
                        c = step[1]
                        t, tile = proj_tile("QK", c)
                        act.wait_ge(proj_full.sem, proj_full.at(n, t + 1))
                        if c == 1:
                            act.wait_ge(spread[0].sem, spread[0].at(n, SPREAD_DMAS))
                        elif c == 2:
                            act.wait_ge(spread[1].sem, spread[1].at(n, SPREAD_DMAS))
                        else:
                            if spread[0].due(n, 0):
                                act.wait_ge(spread[0].sem, spread[0].at(n, 0))
                        act.activation(qk_hi[:, 0, :], tile[:, 0:NODES], ACT.Copy, scale=0.5 * float(H) ** -0.5)
                        act.activation(qk_hi[:, 1, :], tile[:, NODES:2 * NODES], ACT.Copy).then_inc(proj_hi.sem, 1)
                    elif kind == "EX":
                        k = step[1]
                        act.wait_ge(score_free.sem, score_free.at(n, k + 1))
                        if pT_full.due(n, k - 1):
                            act.wait_ge(pT_full.sem, pT_full.at(n, k - 1))
                        for i in range(2):
                            col = 2 * k + i
                            ins = act.activation(prob[:, k % 2, i, :], neg_t[:, k % 2, i, :], ACT.Exp,
                                                 bias=neg_max[:, col:col + 1], scale=-1.0,
                                                 accum_out=row_sum[:, col:col + 1])
                        ins.then_inc(prob_ready.sem, 1)
                    elif kind == "P":
                        k = step[1]
                        c, qb, pr = k // PPC, k % PPC // 2, k % 2
                        act.wait_ge(pT_full.sem, pT_full.at(n, k + 1))
                        if k % PPC == 0:
                            if c:
                                act.wait_ge(proj_full.sem, proj_full.at(n, PROJ["O", c - 1] + 1))
                            else:
                                act.wait_ge(proj_full.sem, proj_full.at(n, PROJ["CT", 1] + 1))
                        act.activation(prob_t[:, :, 2 * pr:2 * pr + 2, qb * P:(qb + 1) * P],
                                       pT_bank[:, :].rearrange("p (a b m) -> p a b m", a=NB, b=2), ACT.Copy)\
                            .then_inc(pT_free.sem, 1)
                    elif kind == "O":
                        c = step[1]
                        t, tile = proj_tile("O", c)
                        act.wait_ge(proj_full.sem, proj_full.at(n, t + 1))
                        if c:
                            act.wait_ge(proj_free.sem, proj_free.at(n, PROJ["O", c - 1] + 1))
                        else:
                            if proj_free.due(n, PROJ["O", KC - 1] + 1 - PROJ_TILES):
                                act.wait_ge(proj_free.sem, proj_free.at(n, PROJ["O", KC - 1] + 1 - PROJ_TILES))
                        act.activation(scale_t[:, :], tile[:, NODES:2 * NODES], ACT.Copy).then_inc(scale_spread.sem, 1)

            later_pieces = list(range(FIRST_WEIGHTS * KC, len(pieces)))
            for i in range(FIRST_WEIGHTS * KC):
                split_piece(i)
            iteration(0, True, False, True)
            iteration(1, True, True, True)
            with act.Fori(2, GRAPHS - 1) as n:
                iteration(n, True, True, True)
            iteration(GRAPHS - 1, True, True, False)
            iteration(GRAPHS, False, True, False)

        @block.vector
        def _(dve):
            def split_piece(i):
                k, c = pieces[i]
                dve.wait_ge(piece_hi, i + 1)
                dve.tensor_tensor(w_lo[k][:, c, :], stages[i % len(stages)], w_hi[k][:, c, :].bitcast(F32),
                                  ALU.subtract).then_inc(piece_lo, 1)

            def pre_norm_stats(n, src, st, mv, var, chain):
                for s in range(NB):
                    dve.bn_stats(st[:, s, :], src[:, s, :]).then_inc(chain.sem, 1)
                for s in range(NB):
                    dve.wait_ge(chain.sem, chain.at(n, s + 1))
                    dve.sem_inc(passed, 1)
                    dve.bn_aggr(mv[:, s, :], st[:, s, :]).then_inc(chain.sem, 1)
                dve.wait_ge(chain.sem, chain.at(n, 4))
                dve.tensor_scalar(var[:, :], mv[:, :, 1:2].rearrange("p s o -> p (s o)"), EPS_PRE, None, ALU.add)\
                    .then_inc(chain.sem, 1)

            def ln_x(n):
                dve.wait_ge(x_loaded.sem, x_loaded.at(n, 1))
                pre_norm_stats(n, x_in, x_stats, x_mv, x_var, x_chain)
                dve.wait_ge(x_rstd_ready.sem, x_rstd_ready.at(n, 1))
                for s in range(NB):
                    dve.tensor_scalar(x_in[:, s, :], x_in[:, s, :], x_mv[:, s, 0:1], x_rstd[:, s:s + 1],
                                      ALU.subtract, ALU.mult).then_inc(x_normed.sem, 1)

            def lo_relu(dst, tile, hi, cols, free):
                dve.scalar_tensor_tensor(out=dst[:, :, cols], in0=tile[:, 0:H].rearrange("p (c m) -> p c m", c=KC),
                                         scalar=0.0, in1=hi[:, :, cols].bitcast(F32),
                                         op0=ALU.max, op1=ALU.subtract).then_inc(free.sem, 1)

            def gnn_norm_stats(n, l, s):
                t, tile = gnn_tile("X", l, s)
                i = NB * l + s
                dve.wait_ge(gnn_full.sem, gnn_full.at(n, t + 1))
                dve.bn_stats(stats[:, s, :], tile[:, 0:H]).then_inc(z_stats.sem, 1)
                dve.tensor_scalar(eps_sum[:, s:s + 1], tile[:, H:H + 1], EPS_SUM, EPS_STD, ALU.add, ALU.mult)\
                    .then_inc(z_eps.sem, 1)
                dve.wait_ge(z_stats.sem, z_stats.at(n, 2 * i + 1))
                dve.sem_inc(passed, 1)
                dve.bn_aggr(mean_var[:, s, :], stats[:, s, :]).then_inc(z_stats.sem, 1)
                dve.wait_ge(z_stats.sem, z_stats.at(n, 2 * i + 2))
                dve.scalar_tensor_tensor(out=z[:, s, :], in0=tile[:, 0:H], scalar=mean_var[:, s, 0:1],
                                         in1=ln_a[l][:, :], op0=ALU.subtract, op1=ALU.mult)\
                    .then_inc(gnn_free.sem, 1)

            def gnn_norm_finish(n, l, s):
                t, _ = gnn_tile("X", l, s)
                i = NB * l + s
                dve.wait_ge(z_std.sem, z_std.at(n, i + 1))
                dve.wait_ge(z_eps.sem, z_eps.at(n, i + 1))
                dve.scalar_tensor_tensor(out=rstd[:, s:s + 1], in0=std[:, s:s + 1], scalar=(H / (H - 1.0)) ** 0.5,
                                         in1=eps_sum[:, s:s + 1], op0=ALU.mult, op1=ALU.add).then_inc(z_den.sem, 1)
                dve.wait_ge(z_den.sem, z_den.at(n, i + 1))
                dve.reciprocal(rstd[:, s:s + 1], rstd[:, s:s + 1]).then_inc(z_inv.sem, 1)
                dve.wait_ge(z_inv.sem, z_inv.at(n, i + 1))
                dve.wait_ge(gnn_free.sem, gnn_free.at(n, t + 1))
                fin = dve.scalar_tensor_tensor(out=z[:, s, :], in0=z[:, s, :], scalar=rstd[:, s:s + 1],
                                               in1=ln_b[l][:, :], op0=ALU.mult, op1=ALU.add)
                if l < LAYERS - 1:
                    fin.then_inc(h_next.sem, 1)
                else:
                    fin.then_inc(z_part.sem, 1)
                    dve.wait_ge(z_part.sem, z_part.at(n, s + 1))
                    dve.wait_ge(xres_loaded.sem, xres_loaded.at(n, 1))
                    dve.wait_ge(acc_ready.sem, acc_ready.at(n, NB))
                    dve.scalar_tensor_tensor(out=x1[:, s, :], in0=z[:, s, :], scalar=0.0, in1=x_res[:, s, :],
                                             op0=ALU.max, op1=ALU.add).then_inc(h_next.sem, 1)

            def iteration(n, gnn, attention, following):
                for step in steps_of(gnn, attention, following):
                    if later_pieces:
                        split_piece(later_pieces.pop(0))
                    kind = step[0]
                    if kind == "CLN":
                        if h_next.due(n, 0):
                            dve.wait_ge(h_next.sem, h_next.at(n, 0))
                        pre_norm_stats(n, x1, c_stats, c_mv, c_var, c_chain)
                    elif kind == "CNORM":
                        dve.wait_ge(c_rstd_ready.sem, c_rstd_ready.at(n, 1))
                        if proj_full.due(n, PROJ["O", KC - 1] + 1 - PROJ_TILES):
                            dve.wait_ge(proj_full.sem, proj_full.at(n, PROJ["O", KC - 1] + 1 - PROJ_TILES))
                        for s in range(NB):
                            dve.tensor_scalar(c_norm[:, s, :], x1[:, s, :], c_mv[:, s, 0:1], c_rstd[:, s:s + 1],
                                              ALU.subtract, ALU.mult).then_inc(c_normed.sem, 1)
                    elif kind == "T":
                        l = step[1]
                        for s in range(NB):
                            _, tile = gnn_tile("T", l, s)
                            dve.wait_ge(gnn_hi.sem, gnn_hi.at(n, SPLITS * l + s + 1))
                            lo_relu(hT_lo, tile, hT_hi, node_cols(s), gnn_free)
                    elif kind == "G":
                        _, l, c = step
                        _, tile = gnn_tile("G", l, c)
                        dve.wait_ge(gnn_hi.sem, gnn_hi.at(n, SPLITS * l + NB + c + 1))
                        dve.tensor_tensor(g_lo[:, c, :], tile[:, :], g_hi[:, c, :].bitcast(F32), ALU.subtract)\
                            .then_inc(gnn_free.sem, 1)
                    elif kind == "H":
                        _, l, s = step
                        t, tile = gnn_tile("H", l, s)
                        dve.wait_ge(gnn_full.sem, gnn_full.at(n, t + 1))
                        dve.tensor_tensor(h_lin[:, s, 0:H], tile[:, 0:H], b_lin[l][:, :], ALU.add)\
                            .then_inc(gnn_free.sem, 1)
                    elif kind == "U":
                        _, l, j = step
                        t, tile = gnn_tile("U", l, j)
                        i = NB * l + j
                        dve.wait_ge(gnn_full.sem, gnn_full.at(n, t + 1))
                        dve.wait_ge(mask_ready.sem, mask_ready.at(n, 1))
                        dve.tensor_tensor(att[:, j, :], tile[:, 0:3 * P], mask[:, j, :], ALU.mult)\
                            .then_inc(gnn_free.sem, 1)
                        dve.wait_ge(gnn_free.sem, gnn_free.at(n, t + 1))
                        dve.tensor_tensor(att[:, j, 0:P], att[:, j, 0:P], att[:, j, 2 * P:3 * P], ALU.add)\
                            .then_inc(u_masked.sem, 1)
                    elif kind == "X":
                        gnn_norm_stats(n, *step[1:])
                    elif kind == "XN":
                        gnn_norm_finish(n, *step[1:])
                    elif kind == "LNX":
                        ln_x(n + 1)
                    elif kind == "CT":
                        for s in range(NB):
                            _, tile = proj_tile("CT", s)
                            dve.wait_ge(proj_hi.sem, proj_hi.at(n, s + 1))
                            lo_relu(cT_lo, tile, cT_hi, slice(s * P, (s + 1) * P), proj_free)
                    elif kind == "QK":
                        c = step[1]
                        _, tile = proj_tile("QK", c)
                        dve.wait_ge(proj_hi.sem, proj_hi.at(n, PROJ_SPLIT["QK", c] + 1))
                        dve.scalar_tensor_tensor(out=qk_lo[:, 0, :], in0=tile[:, 0:NODES], scalar=0.5 * float(H) ** -0.5,
                                                 in1=qk_hi[:, 0, :].bitcast(F32), op0=ALU.mult, op1=ALU.subtract)
                        dve.tensor_tensor(qk_lo[:, 1, :], tile[:, NODES:2 * NODES], qk_hi[:, 1, :].bitcast(F32),
                                          ALU.subtract).then_inc(proj_free.sem, 1)
                    elif kind == "V":
                        s = step[1]
                        t, tile = proj_tile("V", s)
                        dve.wait_ge(proj_full.sem, proj_full.at(n, t + 1))
                        dve.tensor_tensor(v[:, s, :], tile[:, 0:H], b_v[:, :], ALU.add).then_inc(proj_free.sem, 1)
                    elif kind == "S":
                        k = step[1]
                        qb = k % PPC // 2
                        dve.wait_ge(adjc_loaded.sem, adjc_loaded.at(n, 1))
                        dve.sem_inc(passed, 1)
                        if prob_ready.due(n, k - 1):
                            dve.wait_ge(prob_ready.sem, prob_ready.at(n, k - 1))
                            dve.sem_inc(passed, 1)
                        dve.wait_ge(score_full.sem, score_full.at(n, k + 1))
                        dve.sem_inc(passed, 1)
                        for i in range(2):
                            col = 2 * k + i
                            ins = dve.tensor_tensor_reduce(neg_t[:, k % 2, i, :],
                                                           score_bank[k % 2][:, i * NODES:(i + 1) * NODES],
                                                           adj_c[:, qb, :], -2.0, BIG, ALU.add, ALU.min,
                                                           neg_max[:, col:col + 1])
                        ins.then_inc(score_free.sem, 1)
                        dve.wait_ge(score_free.sem, score_free.at(n, k + 1))
                        dve.tensor_reduce(any_t[:, 2 * k:2 * k + 2], neg_t[:, k % 2, :, :], AX.X, ALU.max,
                                          apply_absolute_value=True).then_inc(any_ready.sem, 1)
                    elif kind == "R":
                        c = step[1]
                        cols = slice(2 * PPC * c, 2 * PPC * (c + 1))
                        dve.wait_ge(prob_ready.sem, prob_ready.at(n, PPC * (c + 1)))
                        dve.reciprocal(inv_sum[:, cols], row_sum[:, cols]).then_inc(inv_ready.sem, 1)
                        dve.wait_ge(inv_ready.sem, inv_ready.at(n, c + 1))
                        dve.wait_ge(any_ready.sem, any_ready.at(n, PPC * (c + 1)))
                        dve.scalar_tensor_tensor(out=row_scale[:, cols], in0=any_t[:, cols], scalar=0.0,
                                                 in1=inv_sum[:, cols], op0=ALU.is_gt, op1=ALU.mult)\
                            .then_inc(scale_ready.sem, 1)
                    elif kind == "O":
                        c = step[1]
                        _, tile = proj_tile("O", c)
                        dve.wait_ge(scale_spread.sem, scale_spread.at(n, c + 1))
                        dve.tensor_tensor(o_raw[:, :], tile[:, 0:NODES], scale_t[:, :], ALU.mult)\
                            .then_inc(proj_free.sem, 1)
                        dve.wait_ge(proj_free.sem, proj_free.at(n, PROJ["O", c] + 1))
                        dve.tensor_copy(oT_hi[:, c, :], o_raw[:, :]).then_inc(o_part.sem, 1)
                        dve.wait_ge(o_part.sem, o_part.at(n, c + 1))
                        dve.tensor_tensor(oT_lo[:, c, :], o_raw[:, :], oT_hi[:, c, :].bitcast(F32), ALU.subtract)\
                            .then_inc(o_split.sem, 1)
                    elif kind == "Y":
                        s = step[1]
                        t, tile = proj_tile("Y", s)
                        dve.wait_ge(proj_full.sem, proj_full.at(n, t + 1))
                        dve.wait_ge(acc_ready.sem, acc_ready.at(n, NB))
                        dve.tensor_tensor(acc[:, s, :], tile[:, 0:H], acc[:, s, :], ALU.add)\
                            .then_inc(proj_free.sem, 1)

            dve.wait_ge(consts, 5)
            ln_x(0)
            later_pieces = list(range(FIRST_WEIGHTS * KC, len(pieces)))
            for i in range(FIRST_WEIGHTS * KC):
                split_piece(i)
            vec_loaded_all(dve)
            iteration(0, True, False, True)
            iteration(1, True, True, True)
            with dve.Fori(2, GRAPHS - 1) as n:
                iteration(n, True, True, True)
            iteration(GRAPHS - 1, True, True, False)
            iteration(GRAPHS, False, True, False)

        @block.tensor
        def _(pe):
            def product(dst, stationary, moving, chunks=KC):
                terms = [(c, a, b) for c in range(chunks) for a, b in ((0, 0), (0, 1), (1, 0))]
                for i, (c, a, b) in enumerate(terms):
                    ins = pe.matmul(dst, stationary(a, c), moving(b, c), start=i == 0, stop=i == len(terms) - 1)
                return ins

            hT, cT, gT, oT = (hT_hi, hT_lo), (cT_hi, cT_lo), (g_hi, g_lo), (oT_hi, oT_lo)
            wt = (w_hi, w_lo)

            def iteration(n, gnn, attention, following):
                for step in steps_of(gnn, attention, following):
                    kind = step[0]
                    if kind == "T":
                        l = step[1]
                        for s in range(NB):
                            t, tile = gnn_tile("T", l, s)
                            if l == 0:
                                pe.wait_ge(x_normed.sem, x_normed.at(n, s + 1))
                            else:
                                pe.wait_ge(h_next.sem, h_next.at(n, NB * (l - 1) + s + 1))
                            if gnn_free.due(n, gnn_before(t) + 1):
                                pe.wait_ge(gnn_free.sem, gnn_free.at(n, gnn_before(t) + 1))
                            src = x_in if l == 0 else z
                            for c in range(KC):
                                ins = pe.transpose(tile[:, c * P:(c + 1) * P], src[:, s, c * P:(c + 1) * P], ident[:, :])
                            ins.then_inc(gnn_full.sem, 1)
                    elif kind == "G":
                        _, l, c = step
                        t, tile = gnn_tile("G", l, c)
                        if c == 0:
                            pe.wait_ge(gnn_free.sem, gnn_free.at(n, gnn_tile("T", l, NB - 1)[0] + 1))
                            if isinstance(n, int) and n == 0:
                                pe.wait_ge(piece_lo, FIRST_WEIGHTS * KC * (l + 1))
                        if gnn_free.due(n, gnn_before(t) + 1):
                            pe.wait_ge(gnn_free.sem, gnn_free.at(n, gnn_before(t) + 1))
                        for i, side in enumerate(("left", "right")):
                            ins = product(tile[:, i * NODES:(i + 1) * NODES],
                                          lambda a, k: wt[a][f"{side}{l}"][:, k, c * P:(c + 1) * P],
                                          lambda b, k: hT[b][:, k, :])
                        ins.then_inc(gnn_full.sem, 1)
                    elif kind == "H":
                        _, l, s = step
                        t, tile = gnn_tile("H", l, s)
                        if gnn_free.due(n, gnn_before(t) + 1):
                            pe.wait_ge(gnn_free.sem, gnn_free.at(n, gnn_before(t) + 1))
                        product(tile[:, 0:H], lambda a, k: hT[a][:, k, node_cols(s)],
                                lambda b, k: wt[b][f"lin{l}"][:, k, :]).then_inc(gnn_full.sem, 1)
                    elif kind == "U":
                        _, l, j = step
                        t, tile = gnn_tile("U", l, j)
                        if j == 0:
                            pe.wait_ge(gnn_free.sem, gnn_free.at(n, gnn_tile("G", l, KC - 1)[0] + 1))
                        if gnn_free.due(n, gnn_before(t) + 1):
                            pe.wait_ge(gnn_free.sem, gnn_free.at(n, gnn_before(t) + 1))
                        first = P if j == 0 else 0
                        product(tile[:, 0:3 * P], lambda a, k: hT[a][:, k, node_cols(j)],
                                lambda b, k: gT[b][:, k, first:first + 3 * P]).then_inc(gnn_full.sem, 1)
                    elif kind == "X":
                        _, l, s = step
                        t, tile = gnn_tile("X", l, s)
                        pe.wait_ge(att_ready.sem, att_ready.at(n, NB * (l + 1)))
                        pe.wait_ge(gnn_free.sem, gnn_free.at(n, gnn_tile("H", l, NB - 1)[0] + 1))
                        if gnn_free.due(n, gnn_before(t) + 1):
                            pe.wait_ge(gnn_free.sem, gnn_free.at(n, gnn_before(t) + 1))
                        for j in range(NB):
                            at = (s if j == 0 else 1 - s) * P
                            ins = pe.matmul(tile[:, 0:H + 1], att[:, j, at:at + P], h_lin[:, j, 0:H + 1],
                                            start=j == 0, stop=j == NB - 1)
                        ins.then_inc(gnn_full.sem, 1)
                    elif kind == "CT":
                        for s in range(NB):
                            t, tile = proj_tile("CT", s)
                            pe.wait_ge(c_normed.sem, c_normed.at(n, s + 1))
                            if proj_free.due(n, t - 1):
                                pe.wait_ge(proj_free.sem, proj_free.at(n, t - 1))
                            for c in range(KC):
                                ins = pe.transpose(tile[:, c * P:(c + 1) * P], c_norm[:, s, c * P:(c + 1) * P],
                                                   ident[:, :])
                            ins.then_inc(proj_full.sem, 1)
                    elif kind == "QK":
                        c = step[1]
                        t, tile = proj_tile("QK", c)
                        if proj_free.due(n, t - 1):
                            pe.wait_ge(proj_free.sem, proj_free.at(n, t - 1))
                        if c == 0:
                            pe.wait_ge(proj_free.sem, proj_free.at(n, PROJ["CT", NB - 1] + 1))
                            if isinstance(n, int) and n == 1:
                                pe.wait_ge(piece_lo, len(pieces))
                        for i, key in enumerate(("q", "k")):
                            ins = product(tile[:, i * NODES:(i + 1) * NODES],
                                          lambda a, k: wt[a][key][:, k, c * P:(c + 1) * P],
                                          lambda b, k: cT[b][:, k, :])
                        ins.then_inc(proj_full.sem, 1)
                    elif kind == "V":
                        s = step[1]
                        t, tile = proj_tile("V", s)
                        if proj_free.due(n, t - 1):
                            pe.wait_ge(proj_free.sem, proj_free.at(n, t - 1))
                        product(tile[:, 0:H], lambda a, k: cT[a][:, k, s * P:(s + 1) * P],
                                lambda b, k: wt[b]["v"][:, k, :]).then_inc(proj_full.sem, 1)
                    elif kind == "S":
                        k = step[1]
                        c, qb, pr = k // PPC, k % PPC // 2, k % 2
                        if k % PPC == 0:
                            pe.wait_ge(spread[c % 2].sem, spread[c % 2].at(n, SPREAD_DMAS * (1 + (c == 2))))
                        if score_free.due(n, k - 1):
                            pe.wait_ge(score_free.sem, score_free.at(n, k - 1))
                        at = qb * P
                        for i in range(2):
                            g = 2 * pr + i
                            ins = pe.matmul(score_bank[k % 2][:, i * NODES:(i + 1) * NODES],
                                            q_stack[:, c % 2, g, at:at + P], k_stack[:, c % 2, g, :],
                                            start=True, stop=True)
                        ins.then_inc(score_full.sem, 1)
                    elif kind == "P":
                        k = step[1]
                        pe.wait_ge(prob_ready.sem, prob_ready.at(n, k + 1))
                        if pT_free.due(n, k):
                            pe.wait_ge(pT_free.sem, pT_free.at(n, k))
                        for b in range(NB):
                            for i in range(2):
                                at = (2 * b + i) * P
                                ins = pe.transpose(pT_bank[:, at:at + P], prob[:, k % 2, i, b * P:(b + 1) * P], ident[:, :])
                        ins.then_inc(pT_full.sem, 1)
                    elif kind == "O":
                        c = step[1]
                        t, tile = proj_tile("O", c)
                        pe.wait_ge(scale_ready.sem, scale_ready.at(n, c + 1))
                        pe.wait_ge(pT_free.sem, pT_free.at(n, PPC * (c + 1)))
                        pe.wait_ge(proj_free.sem, proj_free.at(n, PROJ["V", NB - 1] + 1))
                        if proj_free.due(n, t - 1):
                            pe.wait_ge(proj_free.sem, proj_free.at(n, t - 1))
                        for b in range(NB):
                            for g in range(HPC):
                                head = HPC * c + g
                                pe.matmul(tile[g * D:(g + 1) * D, 0:NODES], v[:, b, head * D:(head + 1) * D],
                                          prob_t[:, b, g, :], start=b == 0, stop=b == NB - 1)
                        for qb in range(NB):
                            for g in range(HPC):
                                col = 2 * PPC * c + HPC * qb + g
                                ins = pe.matmul(tile[g * D:(g + 1) * D, NODES + qb * P:NODES + (qb + 1) * P],
                                                row_scale[:, col:col + 1].to_broadcast([P, D]), ident[:, :],
                                                start=True, stop=True)
                        ins.then_inc(proj_full.sem, 1)
                    elif kind == "Y":
                        s = step[1]
                        t, tile = proj_tile("Y", s)
                        pe.wait_ge(o_split.sem, o_split.at(n, KC))
                        if proj_free.due(n, t - 1):
                            pe.wait_ge(proj_free.sem, proj_free.at(n, t - 1))
                        product(tile[:, 0:H], lambda a, k: oT[a][:, k, s * P:(s + 1) * P],
                                lambda b, k: wt[b]["o"][:, k, :]).then_inc(proj_full.sem, 1)

            pe.wait_ge(consts, 5)
            iteration(0, True, False, True)
            iteration(1, True, True, True)
            with pe.Fori(2, GRAPHS - 1) as n:
                iteration(n, True, True, True)
            iteration(GRAPHS - 1, True, True, False)
            iteration(GRAPHS, False, True, False)


def kernel(**inputs):
    import numpy as np
    import concourse.bacc as bacc
    from concourse.bass_utils import run_bass_kernel_spmd

    a = {k: np.asarray(t) for k, t in inputs.items()}
    adj = a["adj"]
    blocks = adj.transpose(0, 2, 1).reshape(GRAPHS, NB, P, NB, P)
    adj_t = np.stack([blocks[:, 0], blocks[:, 1, :, ::-1]], axis=1).reshape(GRAPHS, NB, P, NODES)
    by_feature = np.arange(H).reshape(KC, HPC, D).transpose(0, 2, 1).reshape(-1)
    w = {
        "q": a["L1_gnn_Wq"].T[:, by_feature], "k": a["L1_gnn_Wk"].T[:, by_feature],
        "v": a["L1_gnn_Wv"].T, "o": a["L1_gnn_Wo"].T,
    }
    for l in range(LAYERS):
        w[f"left{l}"], w[f"right{l}"] = a["L0_gnn_W_left"][l], a["L0_gnn_W_right"][l]
        w[f"lin{l}"] = a["L0_gnn_W_lin"][l].T
    arrays = {
        "in_x": a["x"], "in_adj": adj, "in_adj_t": adj_t, "in_w": np.stack([w[k] for k in WEIGHTS]),
        "in_vec": np.concatenate([a["L0_gnn_b_lin"], a["L0_gnn_ln_a"], a["L0_gnn_ln_b"],
                                  a["L1_gnn_bv"][None], a["L1_gnn_bo"][None]]),
    }
    arrays = {k: np.ascontiguousarray(t) for k, t in arrays.items()}
    nc = bacc.Bacc("TRN2", target_bir_lowering=False, num_devices=1)
    args = [nc.dram_tensor(k, t.shape, mybir.dt.from_np(t.dtype), kind="ExternalInput").ap() for k, t in arrays.items()]
    args.append(nc.dram_tensor("out", (GRAPHS, NODES, H), F32, kind="ExternalOutput").ap())
    build(nc, *args)
    return run_bass_kernel_spmd(nc, [arrays], core_ids=[0]).results[0]["out"]
```

```python
from contextlib import ExitStack

import concourse.bass as bass
from concourse import mybir

F32 = mybir.dt.float32
F32R = mybir.dt.float32r
ALU = mybir.AluOpType
ACT = mybir.ActivationFunctionType
AX = mybir.AxisListType

P = 128
GRAPHS, NODES, H = 32, 256, 384
LAYERS, HEADS = 2, 12
D = H // HEADS
KC = H // P
NB = NODES // P
HPC = P // D
PAIRS = HEADS * NB // 2
PPC = PAIRS // KC

EPS_PRE = 1e-5
EPS_STD = 1e-3
EPS_SUM = 1e-10
BIG = 3.4e38

TILE = {"T": 0, "G": NB, "H": NB + KC, "U": 2 * NB + KC, "X": 3 * NB + KC}
LAYER_TILES = 4 * NB + KC
GNN_TILES = LAYERS * LAYER_TILES
GNN_BANKS = 3
SPLITS = NB + KC
PROJ = {("CT", 0): 0, ("CT", 1): 1, ("QK", 0): 2, ("QK", 1): 3, ("V", 0): 4, ("V", 1): 5, ("QK", 2): 6}
OUT = {("O", 0): 0, ("O", 1): 1, ("O", 2): 2, ("Y", 0): 3, ("Y", 1): 4}
PROJ_SPLIT = {("CT", 0): 0, ("CT", 1): 1, ("QK", 0): 2, ("QK", 1): 3, ("QK", 2): 4}
GNN_W = ["left0", "right0", "lin0", "left1", "right1", "lin1"]
WEIGHTS = GNN_W + ["q", "k", "v", "o"]
FIRST_WEIGHTS = 3
SPREAD_DMAS = 2 * P // D


TENSOR_ORDER = (
    ("last", "U", 1, 1), ("last", "P", 0), ("last", "V", 1), ("last", "P", 1), ("last", "X", 1, 0),
    ("last", "X", 1, 1), ("last", "P", 2), ("last", "S", 4), ("last", "S", 5), ("last", "QK", 2), ("last", "P", 3),
    ("T", 0), ("last", "S", 6), ("last", "O", 0), ("G", 0, 0), ("last", "S", 7), ("G", 0, 1), ("last", "P", 4),
    ("G", 0, 2), ("last", "P", 5), ("H", 0, 0), ("H", 0, 1), ("last", "P", 6), ("CT", 0), ("last", "S", 8),
    ("last", "S", 9), ("U", 0, 0), ("CT", 1), ("U", 0, 1), ("last", "S", 10), ("last", "P", 7), ("QK", 0),
    ("last", "P", 8), ("last", "S", 11), ("last", "O", 1), ("X", 0, 0), ("last", "P", 9), ("X", 0, 1),
    ("last", "P", 10), ("QK", 1), ("last", "P", 11), ("last", "O", 2), ("S", 0), ("S", 1), ("T", 1), ("V", 0),
    ("last", "Y", 0), ("G", 1, 0), ("last", "Y", 1), ("G", 1, 1), ("G", 1, 2), ("S", 2), ("H", 1, 0), ("S", 3),
    ("H", 1, 1), ("U", 1, 0),
)
SCALAR_ORDER = (
    ("T", 0), ("last", "EX", 4), ("G", 0, 0), ("last", "EX", 5), ("G", 0, 1), ("last", "P", 4), ("G", 0, 2),
    ("last", "P", 5), ("last", "EX", 6), ("last", "EX", 7), ("CT", 0), ("last", "P", 6), ("CT", 1),
    ("last", "O", 0), ("E", 0, 0), ("last", "EX", 8), ("last", "P", 7), ("last", "EX", 9), ("QK", 0), ("E", 0, 1),
    ("last", "EX", 10), ("last", "P", 8), ("last", "P", 9), ("last", "O", 1), ("last", "EX", 11), ("last", "P", 10),
    ("last", "P", 11), ("QK", 1), ("last", "O", 2), ("T", 1), ("G", 1, 0), ("EX", 0), ("G", 1, 1), ("EX", 1),
    ("G", 1, 2), ("E", 1, 0), ("P", 0), ("E", 1, 1), ("P", 1), ("EX", 2), ("EX", 3), ("P", 2), ("QK", 2), ("P", 3),
)
VECTOR_ORDER = (
    ("last", "A", 1), ("last", "G", 1, 2), ("last", "S", 2), ("last", "A", 2), ("last", "H", 1, 0),
    ("last", "H", 1, 1), ("last", "S", 3), ("last", "A", 3), ("last", "U", 1, 0), ("last", "U", 1, 1),
    ("last", "LNX"), ("last", "V", 1), ("last", "X", 1, 0), ("last", "X", 1, 1), ("last", "S", 4), ("last", "R", 0),
    ("last", "A", 4), ("last", "S", 5), ("T", 0), ("last", "XN", 1, 0), ("last", "QK", 2), ("last", "XN", 1, 1),
    ("last", "A", 5), ("last", "S", 6), ("CLN",), ("G", 0, 0), ("G", 0, 1), ("G", 0, 2), ("last", "A", 6),
    ("last", "S", 7), ("CNORM",), ("last", "A", 7), ("H", 0, 0), ("last", "R", 1), ("CT", 0), ("last", "S", 8),
    ("H", 0, 1), ("U", 0, 0), ("CT", 1), ("last", "S", 9), ("U", 0, 1), ("last", "A", 8), ("last", "O", 0),
    ("last", "S", 10), ("last", "A", 9), ("last", "S", 11), ("QK", 0), ("last", "A", 10), ("X", 0, 0),
    ("last", "A", 11), ("X", 0, 1), ("last", "R", 2), ("last", "O", 1), ("XN", 0, 0), ("XN", 0, 1), ("QK", 1),
    ("last", "O", 2), ("T", 1), ("S", 0), ("last", "Y", 0), ("last", "Y", 1), ("G", 1, 0), ("S", 1), ("V", 0),
    ("G", 1, 1), ("A", 0),
)
GPSIMD_ORDER = (
    ("last", "MASK"), ("last", "E", 0, 0), ("last", "E", 0, 1), ("last", "X", 0, 0), ("last", "X", 0, 1),
    ("last", "ACC"), ("last", "E", 1, 0), ("last", "E", 1, 1), ("last", "LNX"), ("last", "X", 1, 0),
    ("last", "X", 1, 1), ("CLN",),
)
GNN_STEPS = {"MASK", "T", "G", "H", "U", "E", "X", "XN"}


def steps_of(order, n):
    for s in order:
        m, step = (n - 1, s[1:]) if s[0] == "last" else (n, s)
        if step[0] in GNN_STEPS:
            first, end = 0, GRAPHS
        elif step[0] == "LNX":
            first, end = 0, GRAPHS - 1
        else:
            first, end = 1, GRAPHS + 1
        if not isinstance(m, int) or first <= m < end:
            yield m, step


def build(nc, x, adj, adj_t, w, vec, out):
    ctx = ExitStack()
    with ctx:
        def sb(name, shape, dt=F32):
            return ctx.enter_context(nc.sbuf_tensor(name, shape, dt))

        def bank(name):
            return ctx.enter_context(nc.psum_tensor(name, [P, 512], F32))

        passed = ctx.enter_context(nc.semaphore("passed"))

        class Count:

            def __init__(self, name, per, first=0, unit=1):
                self.sem = ctx.enter_context(nc.semaphore(name))
                self.per, self.first, self.unit = per, first, unit

            def at(self, n, k):
                return n * (self.per * self.unit) + (k - self.first * self.per) * self.unit

            def due(self, n, k):
                value = self.at(n, k)
                return not isinstance(value, int) or value > 0

        w_hi = {k: sb(f"w_hi_{k}", [P, KC, H], F32R) for k in WEIGHTS}
        w_lo = {k: sb(f"w_lo_{k}", [P, KC, H], F32R) for k in WEIGHTS}
        ln_a = [sb(f"ln_a{l}", [P, H]) for l in range(LAYERS)]
        ln_b = [sb(f"ln_b{l}", [P, H]) for l in range(LAYERS)]
        b_lin = [sb(f"b_lin{l}", [P, H]) for l in range(LAYERS)]
        b_v = sb("b_v", [P, H])
        b_o = sb("b_o", [P, H])
        ident = sb("ident", [P, P])
        power = sb("power", [P, 2, NB])
        x_in = sb("x_in", [P, NB, H])
        adj_n = sb("adj_n", [P, NB, NODES])
        adj_tr = sb("adj_tr", [P, NB, NODES])
        mask = sb("mask", [P, NB, 3 * P])
        hT_hi = sb("hT_hi", [P, KC, NODES], F32R)
        hT_lo = sb("hT_lo", [P, KC, NODES], F32R)
        g_hi = sb("g_hi", [P, KC, 2 * NODES], F32R)
        g_lo = sb("g_lo", [P, KC, 2 * NODES], F32R)
        h_lin = sb("h_lin", [P, NB, H + 2])
        att = sb("att", [P, NB, 3 * P])
        z = sb("z", [P, NB, H])
        x1 = sb("x1", [P, NB, H])
        stats = sb("stats", [P, NB, 6])
        mean_var = sb("mean_var", [P, NB, 2])
        std = sb("std", [P, NB])
        eps_sum = sb("eps_sum", [P, NB])
        rstd = sb("rstd", [P, NB])
        x_stats = sb("x_stats", [P, NB, 6])
        x_mv = sb("x_mv", [P, NB, 2])
        x_var = sb("x_var", [P, NB])
        x_rstd = sb("x_rstd", [P, NB])
        adj_c = sb("adj_c", [P, NB, NODES])
        c_stats = sb("c_stats", [P, NB, 6])
        c_mv = sb("c_mv", [P, NB, 2])
        c_var = sb("c_var", [P, NB])
        c_rstd = sb("c_rstd", [P, NB])
        c_norm = sb("c_norm", [P, NB, H])
        acc = sb("acc", [P, NB, H])
        cT_hi = sb("cT_hi", [P, KC, NODES], F32R)
        cT_lo = sb("cT_lo", [P, KC, NODES], F32R)
        qk_hi = sb("qk_hi", [P, 2, NODES], F32R)
        qk_lo = sb("qk_lo", [P, 2, NODES], F32R)
        q_stack = sb("q_stack", [P, 2, HPC, NODES], F32R)
        k_stack = sb("k_stack", [P, 2, HPC, NODES], F32R)
        v = sb("v", [P, NB, H])
        neg_t = sb("neg_t", [P, 2, 2, NODES])
        neg_max = sb("neg_max", [P, 2 * PAIRS])
        any_t = sb("any_t", [P, 2 * PAIRS])
        row_sum = sb("row_sum", [P, 2 * PAIRS])
        inv_sum = sb("inv_sum", [P, 2 * PAIRS])
        row_scale = sb("row_scale", [P, 2 * PAIRS])
        prob = sb("prob", [P, 2, 2, NODES])
        prob_t = sb("prob_t", [P, NB, HPC, NODES])
        scale_t = sb("scale_t", [P, NODES])
        o_raw = sb("o_raw", [P, NODES])
        oT_hi = sb("oT_hi", [P, KC, NODES], F32R)
        oT_lo = sb("oT_lo", [P, KC, NODES], F32R)

        gnn_bank = [bank(f"gnn_bank{i}") for i in range(GNN_BANKS)]
        proj_bank, out_bank = bank("proj_bank"), bank("out_bank")
        score_bank = [bank(f"score_bank{i}") for i in range(2)]
        pT_bank = bank("pT_bank")

        vec_loaded = Count("vec_loaded", 0)
        pieces = [(k, c) for k in WEIGHTS for c in range(KC)]
        stages = [prob_t[:, :, :, :].rearrange("p a b c -> p (a b c)")[:, i * H:(i + 1) * H] for i in range(5)]
        piece_loaded = [ctx.enter_context(nc.semaphore(f"piece_loaded{i}")) for i in range(len(stages))]
        piece_hi = ctx.enter_context(nc.semaphore("piece_hi"))
        piece_lo = ctx.enter_context(nc.semaphore("piece_lo"))
        consts = ctx.enter_context(nc.semaphore("consts"))
        x_loaded = Count("x_loaded", 1, unit=16)
        xres_loaded = Count("xres_loaded", 1, unit=16)
        adjn_loaded = Count("adjn_loaded", 1, unit=16)
        adjt_loaded = Count("adjt_loaded", 1, unit=16)
        adjc_loaded = Count("adjc_loaded", 1, first=1, unit=16)
        out_stored = Count("out_stored", 1, first=1, unit=16)
        x_chain = Count("x_chain", 5)
        x_rstd_ready = Count("x_rstd_ready", 1)
        x_normed = Count("x_normed", NB)
        mask_ready = Count("mask_ready", 1)
        mask_part = Count("mask_part", 3 * NB)
        gnn_full = Count("gnn_full", GNN_TILES)
        gnn_free = Count("gnn_free", GNN_TILES)
        gnn_hi = Count("gnn_hi", LAYERS * SPLITS)
        u_masked = Count("u_masked", LAYERS * NB)
        u_exp = Count("u_exp", LAYERS * NB)
        att_ready = Count("att_ready", LAYERS * NB)
        z_stats = Count("z_stats", 2 * LAYERS * NB)
        z_std = Count("z_std", LAYERS * NB)
        z_eps = Count("z_eps", LAYERS * NB)
        z_den = Count("z_den", LAYERS * NB)
        z_inv = Count("z_inv", LAYERS * NB)
        z_part = Count("z_part", NB)
        h_next = Count("h_next", LAYERS * NB)
        c_chain = Count("c_chain", 5, first=1)
        c_rstd_ready = Count("c_rstd_ready", 1, first=1)
        c_normed = Count("c_normed", NB, first=1)
        acc_ready = Count("acc_ready", NB, first=1)
        proj_full = Count("proj_full", len(PROJ), first=1)
        proj_free = Count("proj_free", len(PROJ), first=1)
        out_full = Count("out_full", len(OUT), first=1)
        out_free = Count("out_free", len(OUT), first=1)
        proj_hi = Count("proj_hi", len(PROJ_SPLIT), first=1)
        spread = [Count("spread0", 2 * SPREAD_DMAS, first=1, unit=16), Count("spread1", SPREAD_DMAS, first=1, unit=16)]
        score_full = Count("score_full", PAIRS, first=1)
        score_free = Count("score_free", PAIRS, first=1)
        any_ready = Count("any_ready", PAIRS, first=1)
        prob_ready = Count("prob_ready", PAIRS, first=1)
        pT_full = Count("pT_full", PAIRS, first=1)
        pT_free = Count("pT_free", PAIRS, first=1)
        inv_ready = Count("inv_ready", KC, first=1)
        scale_ready = Count("scale_ready", KC, first=1)
        scale_spread = Count("scale_spread", KC, first=1)
        o_part = Count("o_part", KC, first=1)
        o_split = Count("o_split", KC, first=1)

        def gnn_tile(kind, l, i):
            t = l * LAYER_TILES + TILE[kind] + i
            return t, gnn_bank[t % GNN_BANKS]

        def gnn_before(t):
            if t >= GNN_BANKS:
                return t - GNN_BANKS
            return max(u for u in range(GNN_TILES) if u % GNN_BANKS == t) - GNN_TILES


        def node_cols(s):
            return slice((NB - 1 - s) * P, (NB - s) * P)

        def vec_loaded_all(eng):
            eng.wait_ge(vec_loaded.sem, 16 * 8)

        block = ctx.enter_context(nc.Block())

        @block.sync
        def _(sp):
            def load_piece(i):
                if i >= len(stages):
                    sp.wait_ge(piece_lo, i - len(stages) + 1)
                k, c = pieces[i]
                sp.dma_start(stages[i % len(stages)], w[WEIGHTS.index(k), c * P:(c + 1) * P, :])\
                    .then_inc(piece_loaded[i % len(stages)], 16)

            def load_x(n):
                sp.dma_start(x_in[:, :, :], x[n].rearrange("(s p) h -> p s h", p=P)).then_inc(x_loaded.sem, 16)

            def load_adj(n):
                if mask_ready.due(n, 0):
                    sp.wait_ge(mask_ready.sem, mask_ready.at(n, 0))
                    sp.sem_inc(passed, 1)
                sp.dma_start(adj_n[:, :, :], adj[n].rearrange("(s p) j -> p s j", p=P)).then_inc(adjn_loaded.sem, 16)
                if att_ready.due(n, 0):
                    sp.wait_ge(att_ready.sem, att_ready.at(n, 0))
                    sp.sem_inc(passed, 1)
                sp.dma_start(adj_tr[:, :, :], adj_t[n].rearrange("s p j -> p s j")).then_inc(adjt_loaded.sem, 16)

            def load_residual(n):
                if acc_ready.due(n, NB):
                    sp.wait_ge(acc_ready.sem, acc_ready.at(n, NB))
                    sp.sem_inc(passed, 1)
                    sp.wait_ge(c_normed.sem, c_normed.at(n, NB))
                    sp.sem_inc(passed, 1)
                sp.dma_start(x1[:, :, :], x[n].rearrange("(s p) h -> p s h", p=P)).then_inc(xres_loaded.sem, 16)

            def stack_parts(n, c):
                sp.wait_ge(proj_free.sem, proj_free.at(n, PROJ["QK", c] + 1))
                sp.sem_inc(passed, 1)
                if score_full.due(n, (PAIRS - PAIRS, 2 * PPC - PAIRS, PPC)[c]):
                    sp.wait_ge(score_full.sem, score_full.at(n, (PAIRS - PAIRS, 2 * PPC - PAIRS, PPC)[c]))
                    sp.sem_inc(passed, 1)
                for d in range(P // D):
                    for i, (stack, part) in enumerate(((q_stack, (qk_hi, qk_lo)[d % 2]),
                                                       (k_stack, (qk_hi, qk_lo)[d // 2]))):
                        sp.dma_start(stack[d * D:(d + 1) * D, c % 2, :, :].bitcast(F32), part[:, i, :].bitcast(F32))\
                            .then_inc(spread[c % 2].sem, 16)

            def iteration(n, gnn=True, attention=True, last=True, following=True):
                if gnn:
                    load_adj(n)
                if following:
                    sp.wait_ge(gnn_full.sem, gnn_full.at(n, NB))
                    sp.sem_inc(passed, 1)
                    load_x(n + 1)
                if attention:
                    if score_free.due(n, 0):
                        sp.wait_ge(score_free.sem, score_free.at(n, 0))
                        sp.sem_inc(passed, 1)
                    sp.dma_start(adj_c[:, :, :], adj[n - 1].rearrange("(s p) j -> p s j", p=P))\
                        .then_inc(adjc_loaded.sem, 16)
                    stack_parts(n, 0)
                if last:
                    sp.wait_ge(out_free.sem, out_free.at(n - 1, len(OUT)))
                    sp.sem_inc(passed, 1)
                    sp.dma_start(out[n - 2].rearrange("(s p) h -> p s h", p=P), acc[:, :, :])\
                        .then_inc(out_stored.sem, 16)
                if gnn:
                    load_residual(n)
                if attention:
                    stack_parts(n, 1)
                    stack_parts(n, 2)

            load_x(0)
            for i in range(len(stages)):
                load_piece(i)
            for i, t in enumerate([b_lin[0], b_lin[1], ln_a[0], ln_a[1], ln_b[0], ln_b[1], b_v, b_o]):
                sp.dma_start(t[:, :], vec[i:i + 1, :].to_broadcast([P, H])).then_inc(vec_loaded.sem, 16)
            for i in range(len(stages), FIRST_WEIGHTS * KC):
                load_piece(i)
            load_adj(0)
            load_residual(0)
            for i in range(FIRST_WEIGHTS * KC, len(pieces)):
                load_piece(i)
            sp.wait_ge(gnn_full.sem, gnn_full.at(0, NB))
            sp.sem_inc(passed, 1)
            load_x(1)
            iteration(1, last=False)
            iteration(2)
            with sp.Fori(3, GRAPHS - 1) as n:
                iteration(n)
            iteration(GRAPHS - 1, following=False)
            iteration(GRAPHS, gnn=False, following=False)
            iteration(GRAPHS + 1, gnn=False, attention=False, following=False)
            sp.wait_ge(out_stored.sem, out_stored.at(GRAPHS, 1))
            sp.sem_inc(passed, 1)

        @block.gpsimd
        def _(pool):
            def build_masks(n):
                pool.wait_ge(adjn_loaded.sem, adjn_loaded.at(n, 1))
                pool.sem_inc(passed, 1)
                pool.wait_ge(adjt_loaded.sem, adjt_loaded.at(n, 1))
                pool.sem_inc(passed, 1)
                if gnn_free.due(n, TILE["U"] + NB + LAYER_TILES - GNN_TILES):
                    pool.wait_ge(gnn_free.sem, gnn_free.at(n, TILE["U"] + NB + LAYER_TILES - GNN_TILES))
                    pool.sem_inc(passed, 1)
                for b in range(NB):
                    pool.affine_select(out=mask[:, b, 0:P], in_=adj_tr[:, b, 0:P], compare_op=ALU.is_ge, fill=0.0,
                                       base=0, pattern=[[-1, P]], channel_multiplier=1).then_inc(mask_part.sem, 1)
                    src = adj_n[:, 0, P:2 * P] if b == 0 else adj_tr[:, 1, P:2 * P]
                    pool.tensor_scalar(mask[:, b, P:2 * P], src, 1.0, 0.0, ALU.mult, ALU.add)\
                        .then_inc(mask_part.sem, 1)
                    last = pool.affine_select(out=mask[:, b, 2 * P:3 * P], in_=adj_n[:, b, b * P:(b + 1) * P],
                                              compare_op=ALU.is_ge, fill=0.0, base=-1, pattern=[[1, P]],
                                              channel_multiplier=-1)
                    if b < NB - 1:
                        last.then_inc(mask_part.sem, 1)
                last.then_inc(mask_ready.sem, 1)

            def iteration(n):
                for n, step in steps_of(GPSIMD_ORDER, n):
                    kind = step[0]
                    if kind == "CLN":
                        pool.wait_ge(c_chain.sem, c_chain.at(n, 5))
                        pool.tensor_tensor(c_rstd[:, :], c_var[:, :], power[:, 1, :], ALU.pow)\
                            .then_inc(c_rstd_ready.sem, 1)
                    elif kind == "ACC":
                        if out_stored.due(n, 0):
                            pool.wait_ge(out_stored.sem, out_stored.at(n, 0))
                        for s in range(NB):
                            pool.tensor_tensor(acc[:, s, :], x1[:, s, :], b_o[:, :], ALU.add)\
                                .then_inc(acc_ready.sem, 1)
                    elif kind == "MASK":
                        build_masks(n)
                    elif kind == "E":
                        _, l, j = step
                        pool.wait_ge(u_exp.sem, u_exp.at(n, NB * l + j + 1))
                        pool.tensor_tensor(att[:, j, 0:NODES], att[:, j, 0:NODES], adj_tr[:, j, :], ALU.mult)\
                            .then_inc(att_ready.sem, 1)
                    elif kind == "X":
                        _, l, s = step
                        pool.wait_ge(z_stats.sem, z_stats.at(n, 2 * (NB * l + s) + 2))
                        pool.tensor_tensor(std[:, s:s + 1], mean_var[:, s, 1:2], power[:, 0, 0:1], ALU.pow)\
                            .then_inc(z_std.sem, 1)
                    elif kind == "LNX":
                        ln_x(n + 1)

            def ln_x(n):
                pool.wait_ge(x_chain.sem, x_chain.at(n, 5))
                pool.tensor_tensor(x_rstd[:, :], x_var[:, :], power[:, 1, :], ALU.pow).then_inc(x_rstd_ready.sem, 1)

            pool.memset(power[:, 0, :], 0.5).then_inc(consts, 1)
            pool.memset(power[:, 1, :], -0.5).then_inc(consts, 1)
            pool.memset(h_lin[:, :, H:H + 2], 1.0).then_inc(consts, 1)
            pool.memset(ident[:, :], 0.0).then_inc(consts, 1)
            pool.wait_ge(consts, 4)
            pool.affine_select(out=ident[:, :], in_=ident[:, :], compare_op=ALU.not_equal, fill=1.0, base=0,
                               pattern=[[-1, P]], channel_multiplier=1).then_inc(consts, 1)
            vec_loaded_all(pool)
            ln_x(0)
            iteration(0)
            iteration(1)
            iteration(2)
            with pool.Fori(3, GRAPHS - 1) as n:
                iteration(n)
            iteration(GRAPHS - 1)
            iteration(GRAPHS)
            iteration(GRAPHS + 1)

        @block.scalar
        def _(act):
            def split_piece(i):
                k, c = pieces[i]
                act.wait_ge(piece_loaded[i % len(stages)], 16 * (i // len(stages) + 1))
                act.activation(w_hi[k][:, c, :], stages[i % len(stages)], ACT.Copy).then_inc(piece_hi, 1)

            def transposed_hi(n, l, s):
                t, tile = gnn_tile("T", l, s)
                act.wait_ge(gnn_full.sem, gnn_full.at(n, t + 1))
                act.activation(hT_hi[:, :, node_cols(s)], tile[:, 0:H].rearrange("p (c m) -> p c m", c=KC), ACT.Relu)\
                    .then_inc(gnn_hi.sem, 1)

            def iteration(n):
                for n, step in steps_of(SCALAR_ORDER, n):
                    kind = step[0]
                    if kind == "T":
                        for s in range(NB):
                            transposed_hi(n, step[1], s)
                    elif kind == "G":
                        _, l, c = step
                        t, tile = gnn_tile("G", l, c)
                        act.wait_ge(gnn_full.sem, gnn_full.at(n, t + 1))
                        act.activation(g_hi[:, c, :], tile[:, :], ACT.Copy).then_inc(gnn_hi.sem, 1)
                    elif kind == "E":
                        _, l, j = step
                        act.wait_ge(u_masked.sem, u_masked.at(n, NB * l + j + 1))
                        act.activation(att[:, j, 0:NODES], att[:, j, 0:NODES], ACT.Exp, scale=float(H) ** -0.5)\
                            .then_inc(u_exp.sem, 1)
                    elif kind == "CT":
                        s = step[1]
                        act.wait_ge(proj_full.sem, proj_full.at(n, PROJ[step] + 1))
                        act.activation(cT_hi[:, :, s * P:(s + 1) * P],
                                       proj_bank[:, 0:H].rearrange("p (c m) -> p c m", c=KC), ACT.Relu)\
                            .then_inc(proj_hi.sem, 1)
                    elif kind == "QK":
                        c = step[1]
                        act.wait_ge(proj_full.sem, proj_full.at(n, PROJ[step] + 1))
                        if c == 1:
                            act.wait_ge(spread[0].sem, spread[0].at(n, SPREAD_DMAS))
                        elif c == 2:
                            act.wait_ge(spread[1].sem, spread[1].at(n, SPREAD_DMAS))
                        else:
                            if spread[0].due(n, 0):
                                act.wait_ge(spread[0].sem, spread[0].at(n, 0))
                        act.activation(qk_hi[:, 0, :], proj_bank[:, 0:NODES], ACT.Copy, scale=0.5 * float(H) ** -0.5)
                        act.activation(qk_hi[:, 1, :], proj_bank[:, NODES:2 * NODES], ACT.Copy).then_inc(proj_hi.sem, 1)
                    elif kind == "EX":
                        k = step[1]
                        act.wait_ge(score_free.sem, score_free.at(n, k + 1))
                        if pT_full.due(n, k - 1):
                            act.wait_ge(pT_full.sem, pT_full.at(n, k - 1))
                        for i in range(2):
                            col = 2 * k + i
                            ins = act.activation(prob[:, k % 2, i, :], neg_t[:, k % 2, i, :], ACT.Exp,
                                                 bias=neg_max[:, col:col + 1], scale=-1.0,
                                                 accum_out=row_sum[:, col:col + 1])
                        ins.then_inc(prob_ready.sem, 1)
                    elif kind == "P":
                        k = step[1]
                        c, qb, pr = k // PPC, k % PPC // 2, k % 2
                        act.wait_ge(pT_full.sem, pT_full.at(n, k + 1))
                        if k % PPC == 0 and out_full.due(n, OUT["O", (c - 1) % KC] + 1 - (0 if c else len(OUT))):
                            act.wait_ge(out_full.sem, out_full.at(n, OUT["O", (c - 1) % KC] + 1 - (0 if c else len(OUT))))
                        act.activation(prob_t[:, :, 2 * pr:2 * pr + 2, qb * P:(qb + 1) * P],
                                       pT_bank[:, :].rearrange("p (a b m) -> p a b m", a=NB, b=2), ACT.Copy)\
                            .then_inc(pT_free.sem, 1)
                    elif kind == "O":
                        act.wait_ge(out_full.sem, out_full.at(n, OUT[step] + 1))
                        before = OUT[step] if step[1] else OUT["O", KC - 1] + 1 - len(OUT)
                        if out_free.due(n, before):
                            act.wait_ge(out_free.sem, out_free.at(n, before))
                        act.activation(scale_t[:, :], out_bank[:, NODES:2 * NODES], ACT.Copy)\
                            .then_inc(scale_spread.sem, 1)

            for i in range(FIRST_WEIGHTS * KC):
                split_piece(i)
            iteration(0)
            iteration(1)
            iteration(2)
            with act.Fori(3, GRAPHS - 1) as n:
                iteration(n)
            iteration(GRAPHS - 1)
            iteration(GRAPHS)
            iteration(GRAPHS + 1)

        @block.vector
        def _(dve):
            def split_piece(i):
                k, c = pieces[i]
                dve.wait_ge(piece_hi, i + 1)
                dve.tensor_tensor(w_lo[k][:, c, :], stages[i % len(stages)], w_hi[k][:, c, :].bitcast(F32),
                                  ALU.subtract).then_inc(piece_lo, 1)

            def split_later_piece(i):
                k, c = pieces[i]
                dve.wait_ge(piece_loaded[i % len(stages)], 16 * (i // len(stages) + 1))
                dve.tensor_copy(w_hi[k][:, c, :], stages[i % len(stages)]).then_inc(piece_hi, 1)
                split_piece(i)

            def pre_norm_stats(n, src, st, mv, var, chain):
                for s in range(NB):
                    dve.bn_stats(st[:, s, :], src[:, s, :]).then_inc(chain.sem, 1)
                for s in range(NB):
                    dve.wait_ge(chain.sem, chain.at(n, s + 1))
                    dve.sem_inc(passed, 1)
                    dve.bn_aggr(mv[:, s, :], st[:, s, :]).then_inc(chain.sem, 1)
                dve.wait_ge(chain.sem, chain.at(n, 4))
                dve.tensor_scalar(var[:, :], mv[:, :, 1:2].rearrange("p s o -> p (s o)"), EPS_PRE, None, ALU.add)\
                    .then_inc(chain.sem, 1)

            def ln_x(n):
                dve.wait_ge(x_loaded.sem, x_loaded.at(n, 1))
                pre_norm_stats(n, x_in, x_stats, x_mv, x_var, x_chain)
                dve.wait_ge(x_rstd_ready.sem, x_rstd_ready.at(n, 1))
                for s in range(NB):
                    dve.tensor_scalar(x_in[:, s, :], x_in[:, s, :], x_mv[:, s, 0:1], x_rstd[:, s:s + 1],
                                      ALU.subtract, ALU.mult).then_inc(x_normed.sem, 1)

            def lo_relu(dst, tile, hi, cols, free):
                dve.scalar_tensor_tensor(out=dst[:, :, cols], in0=tile[:, 0:H].rearrange("p (c m) -> p c m", c=KC),
                                         scalar=0.0, in1=hi[:, :, cols].bitcast(F32),
                                         op0=ALU.max, op1=ALU.subtract).then_inc(free.sem, 1)

            def gnn_norm_stats(n, l, s):
                t, tile = gnn_tile("X", l, s)
                i = NB * l + s
                dve.wait_ge(gnn_full.sem, gnn_full.at(n, t + 1))
                dve.bn_stats(stats[:, s, :], tile[:, 0:H]).then_inc(z_stats.sem, 1)
                dve.tensor_scalar(eps_sum[:, s:s + 1], tile[:, H:H + 1], EPS_SUM, EPS_STD, ALU.add, ALU.mult)\
                    .then_inc(z_eps.sem, 1)
                dve.wait_ge(z_stats.sem, z_stats.at(n, 2 * i + 1))
                dve.sem_inc(passed, 1)
                dve.bn_aggr(mean_var[:, s, :], stats[:, s, :]).then_inc(z_stats.sem, 1)
                dve.wait_ge(z_stats.sem, z_stats.at(n, 2 * i + 2))
                dve.scalar_tensor_tensor(out=z[:, s, :], in0=tile[:, 0:H], scalar=mean_var[:, s, 0:1],
                                         in1=ln_a[l][:, :], op0=ALU.subtract, op1=ALU.mult)\
                    .then_inc(gnn_free.sem, 1)

            def gnn_norm_finish(n, l, s):
                t, _ = gnn_tile("X", l, s)
                i = NB * l + s
                dve.wait_ge(z_std.sem, z_std.at(n, i + 1))
                dve.wait_ge(z_eps.sem, z_eps.at(n, i + 1))
                dve.scalar_tensor_tensor(out=rstd[:, s:s + 1], in0=std[:, s:s + 1], scalar=(H / (H - 1.0)) ** 0.5,
                                         in1=eps_sum[:, s:s + 1], op0=ALU.mult, op1=ALU.add).then_inc(z_den.sem, 1)
                dve.wait_ge(z_den.sem, z_den.at(n, i + 1))
                dve.reciprocal(rstd[:, s:s + 1], rstd[:, s:s + 1]).then_inc(z_inv.sem, 1)
                dve.wait_ge(z_inv.sem, z_inv.at(n, i + 1))
                dve.wait_ge(gnn_free.sem, gnn_free.at(n, t + 1))
                fin = dve.scalar_tensor_tensor(out=z[:, s, :], in0=z[:, s, :], scalar=rstd[:, s:s + 1],
                                               in1=ln_b[l][:, :], op0=ALU.mult, op1=ALU.add)
                if l < LAYERS - 1:
                    fin.then_inc(h_next.sem, 1)
                else:
                    fin.then_inc(z_part.sem, 1)
                    dve.wait_ge(z_part.sem, z_part.at(n, s + 1))
                    dve.wait_ge(xres_loaded.sem, xres_loaded.at(n, 1))
                    dve.scalar_tensor_tensor(out=x1[:, s, :], in0=z[:, s, :], scalar=0.0, in1=x1[:, s, :],
                                             op0=ALU.max, op1=ALU.add).then_inc(h_next.sem, 1)

            def iteration(n):
                for n, step in steps_of(VECTOR_ORDER, n):
                    if later_pieces:
                        split_later_piece(later_pieces.pop(0))
                    kind = step[0]
                    if kind == "CLN":
                        if h_next.due(n, 0):
                            dve.wait_ge(h_next.sem, h_next.at(n, 0))
                        pre_norm_stats(n, x1, c_stats, c_mv, c_var, c_chain)
                    elif kind == "CNORM":
                        dve.wait_ge(c_rstd_ready.sem, c_rstd_ready.at(n, 1))
                        for s in range(NB):
                            dve.tensor_scalar(c_norm[:, s, :], x1[:, s, :], c_mv[:, s, 0:1], c_rstd[:, s:s + 1],
                                              ALU.subtract, ALU.mult).then_inc(c_normed.sem, 1)
                    elif kind == "T":
                        l = step[1]
                        for s in range(NB):
                            _, tile = gnn_tile("T", l, s)
                            dve.wait_ge(gnn_hi.sem, gnn_hi.at(n, SPLITS * l + s + 1))
                            lo_relu(hT_lo, tile, hT_hi, node_cols(s), gnn_free)
                    elif kind == "G":
                        _, l, c = step
                        _, tile = gnn_tile("G", l, c)
                        dve.wait_ge(gnn_hi.sem, gnn_hi.at(n, SPLITS * l + NB + c + 1))
                        dve.tensor_tensor(g_lo[:, c, :], tile[:, :], g_hi[:, c, :].bitcast(F32), ALU.subtract)\
                            .then_inc(gnn_free.sem, 1)
                    elif kind == "H":
                        _, l, s = step
                        t, tile = gnn_tile("H", l, s)
                        dve.wait_ge(gnn_full.sem, gnn_full.at(n, t + 1))
                        dve.tensor_tensor(h_lin[:, s, 0:H], tile[:, 0:H], b_lin[l][:, :], ALU.add)\
                            .then_inc(gnn_free.sem, 1)
                    elif kind == "U":
                        _, l, j = step
                        t, tile = gnn_tile("U", l, j)
                        i = NB * l + j
                        dve.wait_ge(gnn_full.sem, gnn_full.at(n, t + 1))
                        dve.wait_ge(mask_ready.sem, mask_ready.at(n, 1))
                        dve.tensor_tensor(att[:, j, :], tile[:, 0:3 * P], mask[:, j, :], ALU.mult)\
                            .then_inc(gnn_free.sem, 1)
                        dve.wait_ge(gnn_free.sem, gnn_free.at(n, t + 1))
                        dve.tensor_tensor(att[:, j, 0:P], att[:, j, 0:P], att[:, j, 2 * P:3 * P], ALU.add)\
                            .then_inc(u_masked.sem, 1)
                    elif kind == "X":
                        gnn_norm_stats(n, *step[1:])
                    elif kind == "XN":
                        gnn_norm_finish(n, *step[1:])
                    elif kind == "LNX":
                        ln_x(n + 1)
                    elif kind == "CT":
                        s = step[1]
                        dve.wait_ge(proj_hi.sem, proj_hi.at(n, PROJ_SPLIT[step] + 1))
                        lo_relu(cT_lo, proj_bank, cT_hi, slice(s * P, (s + 1) * P), proj_free)
                    elif kind == "QK":
                        dve.wait_ge(proj_hi.sem, proj_hi.at(n, PROJ_SPLIT[step] + 1))
                        dve.scalar_tensor_tensor(out=qk_lo[:, 0, :], in0=proj_bank[:, 0:NODES], scalar=0.5 * float(H) ** -0.5,
                                                 in1=qk_hi[:, 0, :].bitcast(F32), op0=ALU.mult, op1=ALU.subtract)
                        dve.tensor_tensor(qk_lo[:, 1, :], proj_bank[:, NODES:2 * NODES], qk_hi[:, 1, :].bitcast(F32),
                                          ALU.subtract).then_inc(proj_free.sem, 1)
                    elif kind == "V":
                        s = step[1]
                        dve.wait_ge(proj_full.sem, proj_full.at(n, PROJ[step] + 1))
                        dve.tensor_tensor(v[:, s, :], proj_bank[:, 0:H], b_v[:, :], ALU.add).then_inc(proj_free.sem, 1)
                    elif kind == "S":
                        k = step[1]
                        qb = k % PPC // 2
                        dve.wait_ge(adjc_loaded.sem, adjc_loaded.at(n, 1))
                        dve.sem_inc(passed, 1)
                        if prob_ready.due(n, k - 1):
                            dve.wait_ge(prob_ready.sem, prob_ready.at(n, k - 1))
                            dve.sem_inc(passed, 1)
                        if any_ready.due(n, k - 1):
                            dve.wait_ge(any_ready.sem, any_ready.at(n, k - 1))
                            dve.sem_inc(passed, 1)
                        dve.wait_ge(score_full.sem, score_full.at(n, k + 1))
                        dve.sem_inc(passed, 1)
                        for i in range(2):
                            col = 2 * k + i
                            ins = dve.tensor_tensor_reduce(neg_t[:, k % 2, i, :],
                                                           score_bank[k % 2][:, i * NODES:(i + 1) * NODES],
                                                           adj_c[:, qb, :], -2.0, BIG, ALU.add, ALU.min,
                                                           neg_max[:, col:col + 1])
                        ins.then_inc(score_free.sem, 1)
                    elif kind == "A":
                        k = step[1]
                        dve.wait_ge(score_free.sem, score_free.at(n, k + 1))
                        dve.tensor_reduce(any_t[:, 2 * k:2 * k + 2], neg_t[:, k % 2, :, :], AX.X, ALU.max,
                                          apply_absolute_value=True).then_inc(any_ready.sem, 1)
                    elif kind == "R":
                        c = step[1]
                        cols = slice(2 * PPC * c, 2 * PPC * (c + 1))
                        dve.wait_ge(prob_ready.sem, prob_ready.at(n, PPC * (c + 1)))
                        dve.reciprocal(inv_sum[:, cols], row_sum[:, cols]).then_inc(inv_ready.sem, 1)
                        dve.wait_ge(inv_ready.sem, inv_ready.at(n, c + 1))
                        dve.wait_ge(any_ready.sem, any_ready.at(n, PPC * (c + 1)))
                        dve.scalar_tensor_tensor(out=row_scale[:, cols], in0=any_t[:, cols], scalar=0.0,
                                                 in1=inv_sum[:, cols], op0=ALU.is_gt, op1=ALU.mult)\
                            .then_inc(scale_ready.sem, 1)
                    elif kind == "O":
                        c = step[1]
                        dve.wait_ge(scale_spread.sem, scale_spread.at(n, c + 1))
                        if o_split.due(n, c):
                            dve.wait_ge(o_split.sem, o_split.at(n, c))
                        dve.tensor_tensor(o_raw[:, :], out_bank[:, 0:NODES], scale_t[:, :], ALU.mult)\
                            .then_inc(out_free.sem, 1)
                        dve.wait_ge(out_free.sem, out_free.at(n, OUT[step] + 1))
                        dve.tensor_copy(oT_hi[:, c, :], o_raw[:, :]).then_inc(o_part.sem, 1)
                        dve.wait_ge(o_part.sem, o_part.at(n, c + 1))
                        dve.tensor_tensor(oT_lo[:, c, :], o_raw[:, :], oT_hi[:, c, :].bitcast(F32), ALU.subtract)\
                            .then_inc(o_split.sem, 1)
                    elif kind == "Y":
                        s = step[1]
                        dve.wait_ge(out_full.sem, out_full.at(n, OUT[step] + 1))
                        dve.wait_ge(acc_ready.sem, acc_ready.at(n, NB))
                        dve.tensor_tensor(acc[:, s, :], out_bank[:, 0:H], acc[:, s, :], ALU.add)\
                            .then_inc(out_free.sem, 1)

            dve.wait_ge(consts, 5)
            ln_x(0)
            later_pieces = list(range(FIRST_WEIGHTS * KC, len(pieces)))
            for i in range(FIRST_WEIGHTS * KC):
                split_piece(i)
            vec_loaded_all(dve)
            iteration(0)
            iteration(1)
            iteration(2)
            with dve.Fori(3, GRAPHS - 1) as n:
                iteration(n)
            iteration(GRAPHS - 1)
            iteration(GRAPHS)
            iteration(GRAPHS + 1)

        @block.tensor
        def _(pe):
            def product(dst, stationary, moving, chunks=KC):
                terms = [(c, a, b) for c in range(chunks) for a, b in ((0, 0), (0, 1), (1, 0))]
                for i, (c, a, b) in enumerate(terms):
                    ins = pe.matmul(dst, stationary(a, c), moving(b, c), start=i == 0, stop=i == len(terms) - 1)
                return ins

            hT, cT, gT, oT = (hT_hi, hT_lo), (cT_hi, cT_lo), (g_hi, g_lo), (oT_hi, oT_lo)
            wt = (w_hi, w_lo)

            def iteration(n):
                for n, step in steps_of(TENSOR_ORDER, n):
                    kind = step[0]
                    if kind == "T":
                        l = step[1]
                        for s in range(NB):
                            t, tile = gnn_tile("T", l, s)
                            if l == 0:
                                pe.wait_ge(x_normed.sem, x_normed.at(n, s + 1))
                            else:
                                pe.wait_ge(h_next.sem, h_next.at(n, NB * (l - 1) + s + 1))
                            if gnn_free.due(n, gnn_before(t) + 1):
                                pe.wait_ge(gnn_free.sem, gnn_free.at(n, gnn_before(t) + 1))
                            src = x_in if l == 0 else z
                            for c in range(KC):
                                ins = pe.transpose(tile[:, c * P:(c + 1) * P], src[:, s, c * P:(c + 1) * P], ident[:, :])
                            ins.then_inc(gnn_full.sem, 1)
                    elif kind == "G":
                        _, l, c = step
                        t, tile = gnn_tile("G", l, c)
                        if c == 0:
                            pe.wait_ge(gnn_free.sem, gnn_free.at(n, gnn_tile("T", l, NB - 1)[0] + 1))
                            if isinstance(n, int) and n == 0:
                                pe.wait_ge(piece_lo, FIRST_WEIGHTS * KC * (l + 1))
                        if gnn_free.due(n, gnn_before(t) + 1):
                            pe.wait_ge(gnn_free.sem, gnn_free.at(n, gnn_before(t) + 1))
                        for i, side in enumerate(("left", "right")):
                            ins = product(tile[:, i * NODES:(i + 1) * NODES],
                                          lambda a, k: wt[a][f"{side}{l}"][:, k, c * P:(c + 1) * P],
                                          lambda b, k: hT[b][:, k, :])
                        ins.then_inc(gnn_full.sem, 1)
                    elif kind == "H":
                        _, l, s = step
                        t, tile = gnn_tile("H", l, s)
                        if gnn_free.due(n, gnn_before(t) + 1):
                            pe.wait_ge(gnn_free.sem, gnn_free.at(n, gnn_before(t) + 1))
                        product(tile[:, 0:H], lambda a, k: hT[a][:, k, node_cols(s)],
                                lambda b, k: wt[b][f"lin{l}"][:, k, :]).then_inc(gnn_full.sem, 1)
                    elif kind == "U":
                        _, l, j = step
                        t, tile = gnn_tile("U", l, j)
                        if j == 0:
                            pe.wait_ge(gnn_free.sem, gnn_free.at(n, gnn_tile("G", l, KC - 1)[0] + 1))
                        if gnn_free.due(n, gnn_before(t) + 1):
                            pe.wait_ge(gnn_free.sem, gnn_free.at(n, gnn_before(t) + 1))
                        first = P if j == 0 else 0
                        product(tile[:, 0:3 * P], lambda a, k: hT[a][:, k, node_cols(j)],
                                lambda b, k: gT[b][:, k, first:first + 3 * P]).then_inc(gnn_full.sem, 1)
                    elif kind == "X":
                        _, l, s = step
                        t, tile = gnn_tile("X", l, s)
                        pe.wait_ge(att_ready.sem, att_ready.at(n, NB * (l + 1)))
                        pe.wait_ge(gnn_free.sem, gnn_free.at(n, gnn_tile("H", l, NB - 1)[0] + 1))
                        if gnn_free.due(n, gnn_before(t) + 1):
                            pe.wait_ge(gnn_free.sem, gnn_free.at(n, gnn_before(t) + 1))
                        for j in range(NB):
                            at = (s if j == 0 else 1 - s) * P
                            ins = pe.matmul(tile[:, 0:H + 1], att[:, j, at:at + P], h_lin[:, j, 0:H + 1],
                                            start=j == 0, stop=j == NB - 1)
                        ins.then_inc(gnn_full.sem, 1)
                    elif kind == "CT":
                        s = step[1]
                        pe.wait_ge(c_normed.sem, c_normed.at(n, s + 1))
                        if proj_free.due(n, PROJ[step]):
                            pe.wait_ge(proj_free.sem, proj_free.at(n, PROJ[step]))
                        for c in range(KC):
                            ins = pe.transpose(proj_bank[:, c * P:(c + 1) * P], c_norm[:, s, c * P:(c + 1) * P],
                                               ident[:, :])
                        ins.then_inc(proj_full.sem, 1)
                    elif kind == "QK":
                        c = step[1]
                        if proj_free.due(n, PROJ[step]):
                            pe.wait_ge(proj_free.sem, proj_free.at(n, PROJ[step]))
                        if c == 0:
                            pe.wait_ge(proj_free.sem, proj_free.at(n, PROJ["CT", NB - 1] + 1))
                            if isinstance(n, int) and n == 1:
                                pe.wait_ge(piece_lo, len(pieces))
                        for i, key in enumerate(("q", "k")):
                            ins = product(proj_bank[:, i * NODES:(i + 1) * NODES],
                                          lambda a, k: wt[a][key][:, k, c * P:(c + 1) * P],
                                          lambda b, k: cT[b][:, k, :])
                        ins.then_inc(proj_full.sem, 1)
                    elif kind == "V":
                        s = step[1]
                        if proj_free.due(n, PROJ[step]):
                            pe.wait_ge(proj_free.sem, proj_free.at(n, PROJ[step]))
                        product(proj_bank[:, 0:H], lambda a, k: cT[a][:, k, s * P:(s + 1) * P],
                                lambda b, k: wt[b]["v"][:, k, :]).then_inc(proj_full.sem, 1)
                    elif kind == "S":
                        k = step[1]
                        c, qb, pr = k // PPC, k % PPC // 2, k % 2
                        if k % PPC == 0:
                            pe.wait_ge(spread[c % 2].sem, spread[c % 2].at(n, SPREAD_DMAS * (1 + (c == 2))))
                        if score_free.due(n, k - 1):
                            pe.wait_ge(score_free.sem, score_free.at(n, k - 1))
                        at = qb * P
                        for i in range(2):
                            g = 2 * pr + i
                            ins = pe.matmul(score_bank[k % 2][:, i * NODES:(i + 1) * NODES],
                                            q_stack[:, c % 2, g, at:at + P], k_stack[:, c % 2, g, :],
                                            start=True, stop=True)
                        ins.then_inc(score_full.sem, 1)
                    elif kind == "P":
                        k = step[1]
                        pe.wait_ge(prob_ready.sem, prob_ready.at(n, k + 1))
                        if pT_free.due(n, k):
                            pe.wait_ge(pT_free.sem, pT_free.at(n, k))
                        for b in range(NB):
                            for i in range(2):
                                at = (2 * b + i) * P
                                ins = pe.transpose(pT_bank[:, at:at + P], prob[:, k % 2, i, b * P:(b + 1) * P], ident[:, :])
                        ins.then_inc(pT_full.sem, 1)
                    elif kind == "O":
                        c = step[1]
                        pe.wait_ge(scale_ready.sem, scale_ready.at(n, c + 1))
                        pe.wait_ge(pT_free.sem, pT_free.at(n, PPC * (c + 1)))
                        pe.wait_ge(proj_free.sem, proj_free.at(n, PROJ["V", NB - 1] + 1))
                        if out_free.due(n, OUT[step]):
                            pe.wait_ge(out_free.sem, out_free.at(n, OUT[step]))
                        for b in range(NB):
                            for g in range(HPC):
                                head = HPC * c + g
                                pe.matmul(out_bank[g * D:(g + 1) * D, 0:NODES], v[:, b, head * D:(head + 1) * D],
                                          prob_t[:, b, g, :], start=b == 0, stop=b == NB - 1)
                        for qb in range(NB):
                            for g in range(HPC):
                                col = 2 * PPC * c + HPC * qb + g
                                ins = pe.matmul(out_bank[g * D:(g + 1) * D, NODES + qb * P:NODES + (qb + 1) * P],
                                                row_scale[:, col:col + 1].to_broadcast([P, D]), ident[:, :],
                                                start=True, stop=True)
                        ins.then_inc(out_full.sem, 1)
                    elif kind == "Y":
                        s = step[1]
                        pe.wait_ge(o_split.sem, o_split.at(n, KC))
                        if out_free.due(n, OUT[step]):
                            pe.wait_ge(out_free.sem, out_free.at(n, OUT[step]))
                        product(out_bank[:, 0:H], lambda a, k: oT[a][:, k, s * P:(s + 1) * P],
                                lambda b, k: wt[b]["o"][:, k, :]).then_inc(out_full.sem, 1)

            pe.wait_ge(consts, 5)
            iteration(0)
            iteration(1)
            iteration(2)
            with pe.Fori(3, GRAPHS - 1) as n:
                iteration(n)
            iteration(GRAPHS - 1)
            iteration(GRAPHS)
            iteration(GRAPHS + 1)


def kernel(**inputs):
    import numpy as np
    import concourse.bacc as bacc
    from concourse.bass_utils import run_bass_kernel_spmd

    a = {k: np.asarray(t) for k, t in inputs.items()}
    adj = a["adj"]
    blocks = adj.transpose(0, 2, 1).reshape(GRAPHS, NB, P, NB, P)
    adj_t = np.stack([blocks[:, 0], blocks[:, 1, :, ::-1]], axis=1).reshape(GRAPHS, NB, P, NODES)
    by_feature = np.arange(H).reshape(KC, HPC, D).transpose(0, 2, 1).reshape(-1)
    w = {
        "q": a["L1_gnn_Wq"].T[:, by_feature], "k": a["L1_gnn_Wk"].T[:, by_feature],
        "v": a["L1_gnn_Wv"].T, "o": a["L1_gnn_Wo"].T,
    }
    for l in range(LAYERS):
        w[f"left{l}"], w[f"right{l}"] = a["L0_gnn_W_left"][l], a["L0_gnn_W_right"][l]
        w[f"lin{l}"] = a["L0_gnn_W_lin"][l].T
    arrays = {
        "in_x": a["x"], "in_adj": adj, "in_adj_t": adj_t, "in_w": np.stack([w[k] for k in WEIGHTS]),
        "in_vec": np.concatenate([a["L0_gnn_b_lin"], a["L0_gnn_ln_a"], a["L0_gnn_ln_b"],
                                  a["L1_gnn_bv"][None], a["L1_gnn_bo"][None]]),
    }
    arrays = {k: np.ascontiguousarray(t) for k, t in arrays.items()}
    nc = bacc.Bacc("TRN2", target_bir_lowering=False, num_devices=1)
    args = [nc.dram_tensor(k, t.shape, mybir.dt.from_np(t.dtype), kind="ExternalInput").ap() for k, t in arrays.items()]
    args.append(nc.dram_tensor("out", (GRAPHS, NODES, H), F32, kind="ExternalOutput").ap())
    build(nc, *args)
    return run_bass_kernel_spmd(nc, [arrays], core_ids=[0]).results[0]["out"]
```

```python
from contextlib import ExitStack

import concourse.bass as bass
from concourse import mybir

F32 = mybir.dt.float32
F32R = mybir.dt.float32r
ALU = mybir.AluOpType
ACT = mybir.ActivationFunctionType
AX = mybir.AxisListType

P = 128
GRAPHS, NODES, H = 32, 256, 384
LAYERS, HEADS = 2, 12
D = H // HEADS
KC = H // P
NB = NODES // P
HPC = P // D
PAIRS = HEADS * NB // 2
PPC = PAIRS // KC

EPS_PRE = 1e-5
EPS_STD = 1e-3
EPS_SUM = 1e-10
BIG = 3.4e38

TILE = {"T": 0, "G": NB, "H": NB + KC, "U": 2 * NB + KC, "X": 3 * NB + KC}
LAYER_TILES = 4 * NB + KC
GNN_TILES = LAYERS * LAYER_TILES
GNN_BANKS = 3
SPLITS = NB + KC
PROJ = {("CT", 0): 0, ("CT", 1): 1, ("QK", 0): 2, ("QK", 1): 3, ("V", 0): 4, ("V", 1): 5, ("QK", 2): 6}
OUT = {("O", 0): 0, ("O", 1): 1, ("O", 2): 2, ("Y", 0): 3, ("Y", 1): 4}
PROJ_SPLIT = {("CT", 0): 0, ("CT", 1): 1, ("QK", 0): 2, ("QK", 1): 3, ("QK", 2): 4}
GNN_W = ["left0", "right0", "lin0", "left1", "right1", "lin1"]
WEIGHTS = GNN_W + ["q", "k", "v", "o"]
FIRST_WEIGHTS = 2
PROB_BUFS = 3
VECTORS = 8
SPREAD_DMAS = P // D


TENSOR_ORDER = (
    ("last", "P", 3), ("T", 0), ("last", "S", 7), ("last", "O", 0), ("G", 0, 0), ("G", 0, 1), ("last", "P", 4),
    ("G", 0, 2), ("last", "P", 5), ("last", "S", 8), ("H", 0, 0), ("last", "S", 9), ("CT", 0), ("H", 0, 1),
    ("last", "P", 6), ("CT", 1), ("last", "S", 10), ("U", 0, 0), ("last", "P", 7), ("last", "S", 11), ("QK", 0),
    ("last", "O", 1), ("last", "P", 8), ("U", 0, 1), ("last", "P", 9), ("QK", 1), ("X", 0, 0), ("last", "P", 10),
    ("X", 0, 1), ("last", "P", 11), ("S", 0), ("S", 1), ("last", "O", 2), ("V", 0), ("S", 2), ("last", "Y", 0),
    ("V", 1), ("S", 3), ("P", 0), ("T", 1), ("last", "Y", 1), ("S", 4), ("G", 1, 0), ("G", 1, 1), ("S", 5),
    ("G", 1, 2), ("H", 1, 0), ("H", 1, 1), ("U", 1, 0), ("U", 1, 1), ("P", 1), ("QK", 2), ("X", 1, 0), ("X", 1, 1),
    ("P", 2), ("S", 6),
)
SCALAR_ORDER = (
    ("last", "P", 1), ("last", "EX", 4), ("last", "QK", 2), ("last", "SC", 3), ("last", "P", 2), ("last", "EX", 5),
    ("last", "P", 3), ("T", 0), ("last", "EX", 6), ("last", "SC", 4), ("G", 0, 0), ("last", "O", 0), ("G", 0, 1),
    ("last", "SC", 5), ("last", "P", 4), ("G", 0, 2), ("last", "EX", 7), ("last", "SC", 6), ("CT", 0),
    ("last", "P", 5), ("last", "EX", 8), ("last", "P", 6), ("last", "SC", 7), ("CT", 1), ("last", "EX", 9),
    ("last", "P", 7), ("last", "SC", 8), ("last", "SC", 9), ("QK", 0), ("last", "EX", 10), ("last", "P", 8),
    ("last", "O", 1), ("E", 0, 0), ("last", "EX", 11), ("E", 0, 1), ("last", "P", 9), ("last", "SC", 10),
    ("last", "SC", 11), ("last", "P", 10), ("QK", 1), ("last", "P", 11), ("last", "O", 2), ("EX", 0), ("SC", 0),
    ("EX", 1), ("T", 1), ("EX", 2), ("G", 1, 0), ("SC", 1), ("P", 0), ("EX", 3), ("G", 1, 1), ("G", 1, 2),
    ("SC", 2), ("E", 1, 0), ("E", 1, 1),
)
VECTOR_ORDER = (
    ("T", 0), ("last", "R", 4), ("last", "XN", 1, 0), ("last", "R", 5), ("last", "RS", 4), ("last", "RS", 5),
    ("last", "XN", 1, 1), ("last", "S", 7), ("CLN",), ("G", 0, 0), ("last", "R", 6), ("last", "A", 6), ("G", 0, 1),
    ("last", "RS", 6), ("CNORM",), ("G", 0, 2), ("last", "S", 8), ("CT", 0), ("last", "A", 7), ("last", "R", 7),
    ("last", "R", 8), ("last", "RS", 7), ("last", "S", 9), ("last", "A", 8), ("CT", 1), ("last", "A", 9),
    ("last", "RS", 8), ("last", "R", 9), ("H", 0, 0), ("last", "RS", 9), ("last", "O", 0), ("last", "S", 10),
    ("H", 0, 1), ("last", "S", 11), ("U", 0, 0), ("QK", 0), ("U", 0, 1), ("last", "R", 10), ("last", "O", 1),
    ("last", "A", 10), ("last", "RS", 10), ("last", "R", 11), ("last", "A", 11), ("last", "RS", 11), ("X", 0, 0),
    ("QK", 1), ("S", 0), ("X", 0, 1), ("last", "O", 2), ("A", 0), ("V", 0), ("R", 0), ("RS", 0), ("S", 1),
    ("XN", 0, 0), ("XN", 0, 1), ("last", "Y", 0), ("S", 2), ("T", 1), ("A", 1), ("A", 2), ("R", 1), ("R", 2),
    ("RS", 1), ("RS", 2), ("S", 3), ("S", 4), ("last", "Y", 1), ("V", 1), ("A", 3), ("G", 1, 0), ("R", 3),
    ("RS", 3), ("S", 5), ("G", 1, 1), ("G", 1, 2), ("A", 4), ("H", 1, 0), ("H", 1, 1), ("U", 1, 0), ("A", 5),
    ("U", 1, 1), ("LNX",), ("X", 1, 0), ("X", 1, 1), ("QK", 2), ("S", 6),
)
GPSIMD_ORDER = (
    ("last", "X", 1, 0), ("last", "X", 1, 1), ("MASK",), ("CLN",), ("E", 0, 0), ("E", 0, 1), ("X", 0, 0),
    ("X", 0, 1), ("ACC",), ("E", 1, 0), ("E", 1, 1), ("LNX",),
)
GNN_STEPS = {"MASK", "T", "G", "H", "U", "E", "X", "XN"}


def steps_of(order, n):
    for s in order:
        m, step = (n - 1, s[1:]) if s[0] == "last" else (n, s)
        if step[0] in GNN_STEPS:
            first, end = 0, GRAPHS
        elif step[0] == "LNX":
            first, end = 0, GRAPHS - 1
        else:
            first, end = 1, GRAPHS + 1
        if not isinstance(m, int) or first <= m < end:
            yield m, step


def build(nc, x, adj, adj_t, w, vec, out):
    ctx = ExitStack()
    with ctx:
        def sb(name, shape, dt=F32):
            return ctx.enter_context(nc.sbuf_tensor(name, shape, dt))

        def bank(name):
            return ctx.enter_context(nc.psum_tensor(name, [P, 512], F32))

        passed = ctx.enter_context(nc.semaphore("passed"))

        class Count:

            def __init__(self, name, per, first=0, unit=1):
                self.sem = ctx.enter_context(nc.semaphore(name))
                self.per, self.first, self.unit = per, first, unit

            def at(self, n, k):
                return n * (self.per * self.unit) + (k - self.first * self.per) * self.unit

            def due(self, n, k):
                value = self.at(n, k)
                return not isinstance(value, int) or value > 0

        w_hi = {k: sb(f"w_hi_{k}", [P, KC, H], F32R) for k in WEIGHTS}
        w_lo = {k: sb(f"w_lo_{k}", [P, KC, H], F32R) for k in WEIGHTS}
        ln_a = [sb(f"ln_a{l}", [P, H]) for l in range(LAYERS)]
        ln_b = [sb(f"ln_b{l}", [P, H]) for l in range(LAYERS)]
        b_lin = [sb(f"b_lin{l}", [P, H]) for l in range(LAYERS)]
        b_v = sb("b_v", [P, H])
        b_o = sb("b_o", [P, H])
        ident = sb("ident", [P, P])
        power = sb("power", [P, 2, NB])
        x_in = sb("x_in", [P, NB, H])
        adj_n = sb("adj_n", [P, NB, NODES])
        adj_tr = sb("adj_tr", [P, NB, NODES])
        mask = sb("mask", [P, NB, 3 * P])
        hT_hi = sb("hT_hi", [P, KC, NODES], F32R)
        hT_lo = sb("hT_lo", [P, KC, NODES], F32R)
        g_hi = sb("g_hi", [P, KC, 2 * NODES], F32R)
        g_lo = sb("g_lo", [P, KC, 2 * NODES], F32R)
        h_lin = sb("h_lin", [P, NB, H + 2])
        att = sb("att", [P, NB, 3 * P])
        z = sb("z", [P, NB, H])
        x1 = sb("x1", [P, NB, H])
        stats = sb("stats", [P, NB, 6])
        mean_var = sb("mean_var", [P, NB, 2])
        std = sb("std", [P, NB])
        eps_sum = sb("eps_sum", [P, NB])
        rstd = sb("rstd", [P, NB])
        x_stats = sb("x_stats", [P, NB, 6])
        x_mv = sb("x_mv", [P, NB, 2])
        x_var = sb("x_var", [P, NB])
        x_rstd = sb("x_rstd", [P, NB])
        adj_c = sb("adj_c", [P, NB, NODES])
        c_stats = sb("c_stats", [P, NB, 6])
        c_mv = sb("c_mv", [P, NB, 2])
        c_var = sb("c_var", [P, NB])
        c_rstd = sb("c_rstd", [P, NB])
        c_norm = sb("c_norm", [P, NB, H])
        acc = sb("acc", [P, NB, H])
        cT_hi = sb("cT_hi", [P, KC, NODES], F32R)
        cT_lo = sb("cT_lo", [P, KC, NODES], F32R)
        qk_parts = sb("qk_parts", [P, 2 * 2, NODES], F32R)
        qk_stack = sb("qk_stack", [P, 2, HPC, 2, NODES], F32R)
        v = sb("v", [P, NB, H])
        neg_t = sb("neg_t", [P, 2, 2, NODES])
        neg_max = sb("neg_max", [P, 2 * PAIRS])
        any_t = sb("any_t", [P, 2 * PAIRS])
        row_sum = sb("row_sum", [P, 2 * PAIRS])
        inv_sum = sb("inv_sum", [P, 2 * PAIRS])
        row_scale = sb("row_scale", [P, 2 * PAIRS])
        prob = sb("prob", [P, PROB_BUFS, 2, NODES])
        prob_t = sb("prob_t", [P, NB, HPC, NODES])
        oT_hi = sb("oT_hi", [P, KC, NODES], F32R)
        oT_lo = sb("oT_lo", [P, KC, NODES], F32R)

        gnn_bank = [bank(f"gnn_bank{i}") for i in range(GNN_BANKS)]
        proj_bank, out_bank = bank("proj_bank"), bank("out_bank")
        score_bank = [bank(f"score_bank{i}") for i in range(2)]
        pT_bank = bank("pT_bank")

        vec_loaded = ctx.enter_context(nc.semaphore("vec_loaded"))
        pieces = [(k, c) for k in WEIGHTS for c in range(KC)]
        stages = [prob_t[:, :, :, :].rearrange("p a b c -> p (a b c)")[:, i * H:(i + 1) * H] for i in range(5)]
        piece_loaded = [ctx.enter_context(nc.semaphore(f"piece_loaded{i}")) for i in range(len(stages))]
        piece_hi = ctx.enter_context(nc.semaphore("piece_hi"))
        piece_lo = ctx.enter_context(nc.semaphore("piece_lo"))
        consts = ctx.enter_context(nc.semaphore("consts"))
        x_loaded = Count("x_loaded", 1, unit=16)
        xres_loaded = Count("xres_loaded", 1, unit=16)
        adjn_loaded = Count("adjn_loaded", 1, unit=16)
        adjt_loaded = Count("adjt_loaded", 1, unit=16)
        adjc_loaded = Count("adjc_loaded", 1, first=1, unit=16)
        out_stored = Count("out_stored", 1, first=1, unit=16)
        x_chain = Count("x_chain", 5)
        x_rstd_ready = Count("x_rstd_ready", 1)
        x_normed = Count("x_normed", NB)
        mask_ready = Count("mask_ready", 1)
        gnn_full = Count("gnn_full", GNN_TILES)
        gnn_free = Count("gnn_free", GNN_TILES)
        gnn_hi = Count("gnn_hi", LAYERS * SPLITS)
        u_masked = Count("u_masked", LAYERS * NB)
        u_exp = Count("u_exp", LAYERS * NB)
        att_ready = Count("att_ready", LAYERS * NB)
        z_stats = Count("z_stats", 2 * LAYERS * NB)
        z_std = Count("z_std", LAYERS * NB)
        z_eps = Count("z_eps", LAYERS * NB)
        z_den = Count("z_den", LAYERS * NB)
        z_inv = Count("z_inv", LAYERS * NB)
        z_part = Count("z_part", NB)
        h_next = Count("h_next", LAYERS * NB)
        c_chain = Count("c_chain", 5, first=1)
        c_rstd_ready = Count("c_rstd_ready", 1, first=1)
        c_normed = Count("c_normed", NB, first=1)
        acc_ready = Count("acc_ready", NB, first=1)
        proj_full = Count("proj_full", len(PROJ), first=1)
        proj_free = Count("proj_free", len(PROJ), first=1)
        out_full = Count("out_full", len(OUT), first=1)
        out_free = Count("out_free", len(OUT), first=1)
        proj_hi = Count("proj_hi", len(PROJ_SPLIT), first=1)
        spread = [Count("spread0", 2 * SPREAD_DMAS, first=1, unit=16), Count("spread1", SPREAD_DMAS, first=1, unit=16)]
        score_full = Count("score_full", PAIRS, first=1)
        score_free = Count("score_free", PAIRS, first=1)
        any_ready = Count("any_ready", PAIRS, first=1)
        exp_ready = Count("exp_ready", PAIRS, first=1)
        inv_ready = Count("inv_ready", PAIRS, first=1)
        scale_ready = Count("scale_ready", PAIRS, first=1)
        prob_ready = Count("prob_ready", PAIRS, first=1)
        pT_full = Count("pT_full", PAIRS, first=1)
        pT_free = Count("pT_free", PAIRS, first=1)
        out_hi = Count("out_hi", KC, first=1)

        def gnn_tile(kind, l, i):
            t = l * LAYER_TILES + TILE[kind] + i
            return t, gnn_bank[t % GNN_BANKS]

        def gnn_before(t):
            if t >= GNN_BANKS:
                return t - GNN_BANKS
            return max(u for u in range(GNN_TILES) if u % GNN_BANKS == t) - GNN_TILES


        def node_cols(s):
            return slice((NB - 1 - s) * P, (NB - s) * P)

        block = ctx.enter_context(nc.Block())

        @block.sync
        def _(sp):
            def load_piece(i):
                if i >= len(stages):
                    sp.wait_ge(piece_lo, i - len(stages) + 1)
                k, c = pieces[i]
                sp.dma_start(stages[i % len(stages)], w[WEIGHTS.index(k), c * P:(c + 1) * P, :])\
                    .then_inc(piece_loaded[i % len(stages)], 16)

            def load_x(n):
                sp.dma_start(x_in[:, :, :], x[n].rearrange("(s p) h -> p s h", p=P)).then_inc(x_loaded.sem, 16)

            def load_adj(n):
                if mask_ready.due(n, 0):
                    sp.wait_ge(mask_ready.sem, mask_ready.at(n, 0))
                    sp.sem_inc(passed, 1)
                sp.dma_start(adj_n[:, :, :], adj[n].rearrange("(s p) j -> p s j", p=P)).then_inc(adjn_loaded.sem, 16)
                if att_ready.due(n, 0):
                    sp.wait_ge(att_ready.sem, att_ready.at(n, 0))
                    sp.sem_inc(passed, 1)
                sp.dma_start(adj_tr[:, :, :], adj_t[n].rearrange("s p j -> p s j")).then_inc(adjt_loaded.sem, 16)

            def load_residual(n):
                if acc_ready.due(n, NB):
                    sp.wait_ge(acc_ready.sem, acc_ready.at(n, NB))
                    sp.sem_inc(passed, 1)
                    sp.wait_ge(c_normed.sem, c_normed.at(n, NB))
                    sp.sem_inc(passed, 1)
                sp.dma_start(x1[:, :, :], x[n].rearrange("(s p) h -> p s h", p=P)).then_inc(xres_loaded.sem, 16)

            def stack_parts(n, c):
                sp.wait_ge(proj_free.sem, proj_free.at(n, PROJ["QK", c] + 1))
                sp.sem_inc(passed, 1)
                if score_full.due(n, (PAIRS - PAIRS, 2 * PPC - PAIRS, PPC)[c]):
                    sp.wait_ge(score_full.sem, score_full.at(n, (PAIRS - PAIRS, 2 * PPC - PAIRS, PPC)[c]))
                    sp.sem_inc(passed, 1)
                for d in range(P // D):
                    q_part, k_part = d % 2, 2 + d // 2
                    sp.dma_start(qk_stack[d * D:(d + 1) * D, c % 2, :, :, :].bitcast(F32),
                                 qk_parts[:, q_part:k_part + 1:k_part - q_part, :].bitcast(F32))\
                        .then_inc(spread[c % 2].sem, 16)

            def iteration(n, gnn=True, attention=True, last=True, following=True):
                if gnn:
                    load_adj(n)
                if following:
                    sp.wait_ge(gnn_full.sem, gnn_full.at(n, NB))
                    sp.sem_inc(passed, 1)
                    load_x(n + 1)
                if attention:
                    if score_free.due(n, 0):
                        sp.wait_ge(score_free.sem, score_free.at(n, 0))
                        sp.sem_inc(passed, 1)
                    sp.dma_start(adj_c[:, :, :], adj[n - 1].rearrange("(s p) j -> p s j", p=P))\
                        .then_inc(adjc_loaded.sem, 16)
                    stack_parts(n, 0)
                    stack_parts(n, 1)
                if last:
                    sp.wait_ge(out_free.sem, out_free.at(n - 1, len(OUT)))
                    sp.sem_inc(passed, 1)
                    sp.dma_start(out[n - 2].rearrange("(s p) h -> p s h", p=P), acc[:, :, :])\
                        .then_inc(out_stored.sem, 16)
                if gnn:
                    load_residual(n)
                if attention:
                    stack_parts(n, 2)

            load_x(0)
            for i in range(len(stages)):
                load_piece(i)
            for i in range(len(stages), 3 * KC):
                load_piece(i)
            for i, t in enumerate([b_lin[0], b_lin[1], ln_a[0], ln_a[1], ln_b[0], ln_b[1], b_v, b_o]):
                sp.dma_start(t[:, :], vec[i:i + 1, :].to_broadcast([P, H])).then_inc(vec_loaded, 16)
            load_adj(0)
            load_residual(0)
            for i in range(3 * KC, len(pieces)):
                load_piece(i)
            sp.wait_ge(gnn_full.sem, gnn_full.at(0, NB))
            sp.sem_inc(passed, 1)
            load_x(1)
            iteration(1, last=False)
            iteration(2)
            with sp.Fori(3, GRAPHS - 1) as n:
                iteration(n)
            iteration(GRAPHS - 1, following=False)
            iteration(GRAPHS, gnn=False, following=False)
            iteration(GRAPHS + 1, gnn=False, attention=False, following=False)
            sp.wait_ge(out_stored.sem, out_stored.at(GRAPHS, 1))
            sp.sem_inc(passed, 1)

        @block.gpsimd
        def _(pool):
            def build_masks(n):
                pool.wait_ge(adjn_loaded.sem, adjn_loaded.at(n, 1))
                pool.sem_inc(passed, 1)
                pool.wait_ge(adjt_loaded.sem, adjt_loaded.at(n, 1))
                pool.sem_inc(passed, 1)
                if gnn_free.due(n, TILE["U"] + NB + LAYER_TILES - GNN_TILES):
                    pool.wait_ge(gnn_free.sem, gnn_free.at(n, TILE["U"] + NB + LAYER_TILES - GNN_TILES))
                    pool.sem_inc(passed, 1)
                for b in range(NB):
                    pool.affine_select(out=mask[:, b, 0:P], in_=adj_tr[:, b, 0:P], compare_op=ALU.is_ge, fill=0.0,
                                       base=0, pattern=[[-1, P]], channel_multiplier=1)
                    src = adj_n[:, 0, P:2 * P] if b == 0 else adj_tr[:, 1, P:2 * P]
                    pool.tensor_scalar(mask[:, b, P:2 * P], src, 1.0, 0.0, ALU.mult, ALU.add)
                    last = pool.affine_select(out=mask[:, b, 2 * P:3 * P], in_=adj_n[:, b, b * P:(b + 1) * P],
                                              compare_op=ALU.is_ge, fill=0.0, base=-1, pattern=[[1, P]],
                                              channel_multiplier=-1)
                last.then_inc(mask_ready.sem, 1)

            def iteration(n):
                for n, step in steps_of(GPSIMD_ORDER, n):
                    kind = step[0]
                    if kind == "CLN":
                        pool.wait_ge(c_chain.sem, c_chain.at(n, 5))
                        pool.tensor_tensor(c_rstd[:, :], c_var[:, :], power[:, 1, :], ALU.pow)\
                            .then_inc(c_rstd_ready.sem, 1)
                    elif kind == "ACC":
                        if isinstance(n, int) and n == 1:
                            pool.wait_ge(vec_loaded, 16 * VECTORS)
                        if out_stored.due(n, 0):
                            pool.wait_ge(out_stored.sem, out_stored.at(n, 0))
                        for s in range(NB):
                            pool.tensor_tensor(acc[:, s, :], x1[:, s, :], b_o[:, :], ALU.add)\
                                .then_inc(acc_ready.sem, 1)
                    elif kind == "MASK":
                        build_masks(n)
                    elif kind == "E":
                        _, l, j = step
                        pool.wait_ge(u_exp.sem, u_exp.at(n, NB * l + j + 1))
                        pool.tensor_tensor(att[:, j, 0:NODES], att[:, j, 0:NODES], adj_tr[:, j, :], ALU.mult)\
                            .then_inc(att_ready.sem, 1)
                    elif kind == "X":
                        _, l, s = step
                        pool.wait_ge(z_stats.sem, z_stats.at(n, 2 * (NB * l + s) + 2))
                        pool.tensor_tensor(std[:, s:s + 1], mean_var[:, s, 1:2], power[:, 0, 0:1], ALU.pow)\
                            .then_inc(z_std.sem, 1)
                    elif kind == "LNX":
                        ln_x(n + 1)

            def ln_x(n):
                pool.wait_ge(x_chain.sem, x_chain.at(n, 5))
                pool.tensor_tensor(x_rstd[:, :], x_var[:, :], power[:, 1, :], ALU.pow).then_inc(x_rstd_ready.sem, 1)

            pool.memset(power[:, 0, :], 0.5).then_inc(consts, 1)
            pool.memset(power[:, 1, :], -0.5).then_inc(consts, 1)
            pool.memset(h_lin[:, :, H:H + 2], 1.0).then_inc(consts, 1)
            pool.memset(ident[:, :], 0.0).then_inc(consts, 1)
            pool.wait_ge(consts, 4)
            pool.affine_select(out=ident[:, :], in_=ident[:, :], compare_op=ALU.not_equal, fill=1.0, base=0,
                               pattern=[[-1, P]], channel_multiplier=1).then_inc(consts, 1)
            ln_x(0)
            iteration(0)
            iteration(1)
            iteration(2)
            with pool.Fori(3, GRAPHS - 1) as n:
                iteration(n)
            iteration(GRAPHS - 1)
            iteration(GRAPHS)
            iteration(GRAPHS + 1)

        @block.scalar
        def _(act):
            def split_piece(i):
                k, c = pieces[i]
                act.wait_ge(piece_loaded[i % len(stages)], 16 * (i // len(stages) + 1))
                act.activation(w_hi[k][:, c, :], stages[i % len(stages)], ACT.Copy).then_inc(piece_hi, 1)

            def transposed_hi(n, l, s):
                t, tile = gnn_tile("T", l, s)
                act.wait_ge(gnn_full.sem, gnn_full.at(n, t + 1))
                act.activation(hT_hi[:, :, node_cols(s)], tile[:, 0:H].rearrange("p (c m) -> p c m", c=KC), ACT.Relu)\
                    .then_inc(gnn_hi.sem, 1)

            def iteration(n):
                for n, step in steps_of(SCALAR_ORDER, n):
                    kind = step[0]
                    if kind == "T":
                        for s in range(NB):
                            transposed_hi(n, step[1], s)
                    elif kind == "G":
                        _, l, c = step
                        t, tile = gnn_tile("G", l, c)
                        act.wait_ge(gnn_full.sem, gnn_full.at(n, t + 1))
                        act.activation(g_hi[:, c, :], tile[:, :], ACT.Copy).then_inc(gnn_hi.sem, 1)
                    elif kind == "E":
                        _, l, j = step
                        act.wait_ge(u_masked.sem, u_masked.at(n, NB * l + j + 1))
                        act.activation(att[:, j, 0:NODES], att[:, j, 0:NODES], ACT.Exp, scale=float(H) ** -0.5)\
                            .then_inc(u_exp.sem, 1)
                    elif kind == "CT":
                        s = step[1]
                        act.wait_ge(proj_full.sem, proj_full.at(n, PROJ[step] + 1))
                        act.activation(cT_hi[:, :, s * P:(s + 1) * P],
                                       proj_bank[:, 0:H].rearrange("p (c m) -> p c m", c=KC), ACT.Relu)\
                            .then_inc(proj_hi.sem, 1)
                    elif kind == "QK":
                        c = step[1]
                        act.wait_ge(proj_full.sem, proj_full.at(n, PROJ[step] + 1))
                        if c == 1:
                            act.wait_ge(spread[0].sem, spread[0].at(n, SPREAD_DMAS))
                        elif c == 2:
                            act.wait_ge(spread[1].sem, spread[1].at(n, SPREAD_DMAS))
                        else:
                            if spread[0].due(n, 0):
                                act.wait_ge(spread[0].sem, spread[0].at(n, 0))
                        act.activation(qk_parts[:, 0, :], proj_bank[:, 0:NODES], ACT.Copy, scale=0.5 * float(H) ** -0.5)
                        act.activation(qk_parts[:, 2, :], proj_bank[:, NODES:2 * NODES], ACT.Copy)\
                            .then_inc(proj_hi.sem, 1)
                    elif kind == "EX":
                        k = step[1]
                        act.wait_ge(score_free.sem, score_free.at(n, k + 1))
                        if pT_full.due(n, k + 1 - PROB_BUFS):
                            act.wait_ge(pT_full.sem, pT_full.at(n, k + 1 - PROB_BUFS))
                        for i in range(2):
                            col = 2 * k + i
                            ins = act.activation(prob[:, k % PROB_BUFS, i, :], neg_t[:, k % 2, i, :], ACT.Exp,
                                                 bias=neg_max[:, col:col + 1], scale=-1.0,
                                                 accum_out=row_sum[:, col:col + 1])
                        ins.then_inc(exp_ready.sem, 1)
                    elif kind == "SC":
                        k = step[1]
                        act.wait_ge(scale_ready.sem, scale_ready.at(n, k + 1))
                        for i in range(2):
                            col = 2 * k + i
                            ins = act.activation(prob[:, k % PROB_BUFS, i, :], prob[:, k % PROB_BUFS, i, :], ACT.Copy,
                                                 scale=row_scale[:, col:col + 1])
                        ins.then_inc(prob_ready.sem, 1)
                    elif kind == "P":
                        k = step[1]
                        c, qb, pr = k // PPC, k % PPC // 2, k % 2
                        act.wait_ge(pT_full.sem, pT_full.at(n, k + 1))
                        used = OUT["O", c - 1] + 1 if c else OUT["O", KC - 1] + 1 - len(OUT)
                        if k % PPC == 0 and out_full.due(n, used):
                            act.wait_ge(out_full.sem, out_full.at(n, used))
                        act.activation(prob_t[:, :, 2 * pr:2 * pr + 2, qb * P:(qb + 1) * P],
                                       pT_bank[:, :].rearrange("p (a b m) -> p a b m", a=NB, b=2), ACT.Copy)\
                            .then_inc(pT_free.sem, 1)
                    elif kind == "O":
                        act.wait_ge(out_full.sem, out_full.at(n, OUT[step] + 1))
                        act.activation(oT_hi[:, step[1], :], out_bank[:, 0:NODES], ACT.Copy).then_inc(out_hi.sem, 1)

            for i in range(FIRST_WEIGHTS * KC):
                split_piece(i)
            iteration(0)
            iteration(1)
            iteration(2)
            with act.Fori(3, GRAPHS - 1) as n:
                iteration(n)
            iteration(GRAPHS - 1)
            iteration(GRAPHS)
            iteration(GRAPHS + 1)

        @block.vector
        def _(dve):
            def split_piece(i):
                k, c = pieces[i]
                dve.wait_ge(piece_hi, i + 1)
                dve.tensor_tensor(w_lo[k][:, c, :], stages[i % len(stages)], w_hi[k][:, c, :].bitcast(F32),
                                  ALU.subtract).then_inc(piece_lo, 1)

            def split_later_piece(i):
                k, c = pieces[i]
                dve.wait_ge(piece_loaded[i % len(stages)], 16 * (i // len(stages) + 1))
                dve.tensor_copy(w_hi[k][:, c, :], stages[i % len(stages)]).then_inc(piece_hi, 1)
                split_piece(i)

            def pre_norm_stats(n, src, st, mv, var, chain):
                for s in range(NB):
                    dve.bn_stats(st[:, s, :], src[:, s, :]).then_inc(chain.sem, 1)
                for s in range(NB):
                    dve.wait_ge(chain.sem, chain.at(n, s + 1))
                    dve.sem_inc(passed, 1)
                    dve.bn_aggr(mv[:, s, :], st[:, s, :]).then_inc(chain.sem, 1)
                dve.wait_ge(chain.sem, chain.at(n, 4))
                dve.tensor_scalar(var[:, :], mv[:, :, 1:2].rearrange("p s o -> p (s o)"), EPS_PRE, None, ALU.add)\
                    .then_inc(chain.sem, 1)

            def ln_x(n):
                dve.wait_ge(x_loaded.sem, x_loaded.at(n, 1))
                pre_norm_stats(n, x_in, x_stats, x_mv, x_var, x_chain)
                dve.wait_ge(x_rstd_ready.sem, x_rstd_ready.at(n, 1))
                for s in range(NB):
                    dve.tensor_scalar(x_in[:, s, :], x_in[:, s, :], x_mv[:, s, 0:1], x_rstd[:, s:s + 1],
                                      ALU.subtract, ALU.mult).then_inc(x_normed.sem, 1)

            def lo_relu(dst, tile, hi, cols, free):
                dve.scalar_tensor_tensor(out=dst[:, :, cols], in0=tile[:, 0:H].rearrange("p (c m) -> p c m", c=KC),
                                         scalar=0.0, in1=hi[:, :, cols].bitcast(F32),
                                         op0=ALU.max, op1=ALU.subtract).then_inc(free.sem, 1)

            def gnn_norm_stats(n, l, s):
                t, tile = gnn_tile("X", l, s)
                i = NB * l + s
                dve.wait_ge(gnn_full.sem, gnn_full.at(n, t + 1))
                dve.bn_stats(stats[:, s, :], tile[:, 0:H]).then_inc(z_stats.sem, 1)
                dve.tensor_scalar(eps_sum[:, s:s + 1], tile[:, H:H + 1], EPS_SUM, EPS_STD, ALU.add, ALU.mult)\
                    .then_inc(z_eps.sem, 1)
                dve.wait_ge(z_stats.sem, z_stats.at(n, 2 * i + 1))
                dve.sem_inc(passed, 1)
                dve.bn_aggr(mean_var[:, s, :], stats[:, s, :]).then_inc(z_stats.sem, 1)
                dve.wait_ge(z_stats.sem, z_stats.at(n, 2 * i + 2))
                dve.scalar_tensor_tensor(out=z[:, s, :], in0=tile[:, 0:H], scalar=mean_var[:, s, 0:1],
                                         in1=ln_a[l][:, :], op0=ALU.subtract, op1=ALU.mult)\
                    .then_inc(gnn_free.sem, 1)

            def gnn_norm_finish(n, l, s):
                t, _ = gnn_tile("X", l, s)
                i = NB * l + s
                dve.wait_ge(z_std.sem, z_std.at(n, i + 1))
                dve.wait_ge(z_eps.sem, z_eps.at(n, i + 1))
                dve.scalar_tensor_tensor(out=rstd[:, s:s + 1], in0=std[:, s:s + 1], scalar=(H / (H - 1.0)) ** 0.5,
                                         in1=eps_sum[:, s:s + 1], op0=ALU.mult, op1=ALU.add).then_inc(z_den.sem, 1)
                dve.wait_ge(z_den.sem, z_den.at(n, i + 1))
                dve.reciprocal(rstd[:, s:s + 1], rstd[:, s:s + 1]).then_inc(z_inv.sem, 1)
                dve.wait_ge(z_inv.sem, z_inv.at(n, i + 1))
                dve.wait_ge(gnn_free.sem, gnn_free.at(n, t + 1))
                fin = dve.scalar_tensor_tensor(out=z[:, s, :], in0=z[:, s, :], scalar=rstd[:, s:s + 1],
                                               in1=ln_b[l][:, :], op0=ALU.mult, op1=ALU.add)
                if l < LAYERS - 1:
                    fin.then_inc(h_next.sem, 1)
                else:
                    fin.then_inc(z_part.sem, 1)
                    dve.wait_ge(z_part.sem, z_part.at(n, s + 1))
                    dve.wait_ge(xres_loaded.sem, xres_loaded.at(n, 1))
                    dve.scalar_tensor_tensor(out=x1[:, s, :], in0=z[:, s, :], scalar=0.0, in1=x1[:, s, :],
                                             op0=ALU.max, op1=ALU.add).then_inc(h_next.sem, 1)

            def iteration(n):
                for n, step in steps_of(VECTOR_ORDER, n):
                    if later_pieces:
                        split_later_piece(later_pieces.pop(0))
                    kind = step[0]
                    if kind == "CLN":
                        if h_next.due(n, 0):
                            dve.wait_ge(h_next.sem, h_next.at(n, 0))
                        pre_norm_stats(n, x1, c_stats, c_mv, c_var, c_chain)
                    elif kind == "CNORM":
                        dve.wait_ge(c_rstd_ready.sem, c_rstd_ready.at(n, 1))
                        for s in range(NB):
                            dve.tensor_scalar(c_norm[:, s, :], x1[:, s, :], c_mv[:, s, 0:1], c_rstd[:, s:s + 1],
                                              ALU.subtract, ALU.mult).then_inc(c_normed.sem, 1)
                    elif kind == "T":
                        l = step[1]
                        for s in range(NB):
                            _, tile = gnn_tile("T", l, s)
                            dve.wait_ge(gnn_hi.sem, gnn_hi.at(n, SPLITS * l + s + 1))
                            lo_relu(hT_lo, tile, hT_hi, node_cols(s), gnn_free)
                    elif kind == "G":
                        _, l, c = step
                        _, tile = gnn_tile("G", l, c)
                        dve.wait_ge(gnn_hi.sem, gnn_hi.at(n, SPLITS * l + NB + c + 1))
                        dve.tensor_tensor(g_lo[:, c, :], tile[:, :], g_hi[:, c, :].bitcast(F32), ALU.subtract)\
                            .then_inc(gnn_free.sem, 1)
                    elif kind == "H":
                        _, l, s = step
                        t, tile = gnn_tile("H", l, s)
                        dve.wait_ge(gnn_full.sem, gnn_full.at(n, t + 1))
                        if isinstance(n, int) and n == 0:
                            dve.wait_ge(vec_loaded, 16 * VECTORS)
                        dve.tensor_tensor(h_lin[:, s, 0:H], tile[:, 0:H], b_lin[l][:, :], ALU.add)\
                            .then_inc(gnn_free.sem, 1)
                    elif kind == "U":
                        _, l, j = step
                        t, tile = gnn_tile("U", l, j)
                        i = NB * l + j
                        dve.wait_ge(gnn_full.sem, gnn_full.at(n, t + 1))
                        dve.wait_ge(mask_ready.sem, mask_ready.at(n, 1))
                        dve.tensor_tensor(att[:, j, :], tile[:, 0:3 * P], mask[:, j, :], ALU.mult)\
                            .then_inc(gnn_free.sem, 1)
                        dve.wait_ge(gnn_free.sem, gnn_free.at(n, t + 1))
                        dve.tensor_tensor(att[:, j, 0:P], att[:, j, 0:P], att[:, j, 2 * P:3 * P], ALU.add)\
                            .then_inc(u_masked.sem, 1)
                    elif kind == "X":
                        gnn_norm_stats(n, *step[1:])
                    elif kind == "XN":
                        gnn_norm_finish(n, *step[1:])
                    elif kind == "LNX":
                        ln_x(n + 1)
                    elif kind == "CT":
                        s = step[1]
                        dve.wait_ge(proj_hi.sem, proj_hi.at(n, PROJ_SPLIT[step] + 1))
                        lo_relu(cT_lo, proj_bank, cT_hi, slice(s * P, (s + 1) * P), proj_free)
                    elif kind == "QK":
                        dve.wait_ge(proj_hi.sem, proj_hi.at(n, PROJ_SPLIT[step] + 1))
                        dve.scalar_tensor_tensor(out=qk_parts[:, 1, :], in0=proj_bank[:, 0:NODES],
                                                 scalar=0.5 * float(H) ** -0.5, in1=qk_parts[:, 0, :].bitcast(F32), op0=ALU.mult, op1=ALU.subtract)
                        dve.tensor_tensor(qk_parts[:, 3, :], proj_bank[:, NODES:2 * NODES], qk_parts[:, 2, :].bitcast(F32),
                                          ALU.subtract).then_inc(proj_free.sem, 1)
                    elif kind == "V":
                        s = step[1]
                        dve.wait_ge(proj_full.sem, proj_full.at(n, PROJ[step] + 1))
                        dve.tensor_tensor(v[:, s, :], proj_bank[:, 0:H], b_v[:, :], ALU.add).then_inc(proj_free.sem, 1)
                    elif kind == "S":
                        k = step[1]
                        qb = k % PPC // 2
                        dve.wait_ge(adjc_loaded.sem, adjc_loaded.at(n, 1))
                        dve.sem_inc(passed, 1)
                        if exp_ready.due(n, k - 1):
                            dve.wait_ge(exp_ready.sem, exp_ready.at(n, k - 1))
                            dve.sem_inc(passed, 1)
                        if any_ready.due(n, k - 1):
                            dve.wait_ge(any_ready.sem, any_ready.at(n, k - 1))
                            dve.sem_inc(passed, 1)
                        dve.wait_ge(score_full.sem, score_full.at(n, k + 1))
                        dve.sem_inc(passed, 1)
                        for i in range(2):
                            col = 2 * k + i
                            ins = dve.tensor_tensor_reduce(neg_t[:, k % 2, i, :],
                                                           score_bank[k % 2][:, i * NODES:(i + 1) * NODES],
                                                           adj_c[:, qb, :], -2.0, BIG, ALU.add, ALU.min,
                                                           neg_max[:, col:col + 1])
                        ins.then_inc(score_free.sem, 1)
                    elif kind == "A":
                        k = step[1]
                        dve.wait_ge(score_free.sem, score_free.at(n, k + 1))
                        dve.tensor_reduce(any_t[:, 2 * k:2 * k + 2], neg_t[:, k % 2, :, :], AX.X, ALU.max,
                                          apply_absolute_value=True).then_inc(any_ready.sem, 1)
                    elif kind == "R":
                        k = step[1]
                        cols = slice(2 * k, 2 * k + 2)
                        dve.wait_ge(exp_ready.sem, exp_ready.at(n, k + 1))
                        dve.reciprocal(inv_sum[:, cols], row_sum[:, cols]).then_inc(inv_ready.sem, 1)
                    elif kind == "RS":
                        k = step[1]
                        cols = slice(2 * k, 2 * k + 2)
                        dve.wait_ge(inv_ready.sem, inv_ready.at(n, k + 1))
                        dve.wait_ge(any_ready.sem, any_ready.at(n, k + 1))
                        dve.scalar_tensor_tensor(out=row_scale[:, cols], in0=any_t[:, cols], scalar=0.0,
                                                 in1=inv_sum[:, cols], op0=ALU.is_gt, op1=ALU.mult)\
                            .then_inc(scale_ready.sem, 1)
                    elif kind == "O":
                        c = step[1]
                        dve.wait_ge(out_hi.sem, out_hi.at(n, c + 1))
                        dve.tensor_tensor(oT_lo[:, c, :], out_bank[:, 0:NODES], oT_hi[:, c, :].bitcast(F32),
                                          ALU.subtract).then_inc(out_free.sem, 1)
                    elif kind == "Y":
                        s = step[1]
                        dve.wait_ge(out_full.sem, out_full.at(n, OUT[step] + 1))
                        dve.wait_ge(acc_ready.sem, acc_ready.at(n, NB))
                        dve.tensor_tensor(acc[:, s, :], out_bank[:, 0:H], acc[:, s, :], ALU.add)\
                            .then_inc(out_free.sem, 1)

            dve.wait_ge(consts, 5)
            ln_x(0)
            later_pieces = list(range(FIRST_WEIGHTS * KC, len(pieces)))
            for i in range(FIRST_WEIGHTS * KC):
                split_piece(i)
            iteration(0)
            iteration(1)
            iteration(2)
            with dve.Fori(3, GRAPHS - 1) as n:
                iteration(n)
            iteration(GRAPHS - 1)
            iteration(GRAPHS)
            iteration(GRAPHS + 1)

        @block.tensor
        def _(pe):
            def product(dst, stationary, moving, chunks=KC):
                terms = [(c, a, b) for c in range(chunks) for a, b in ((0, 0), (0, 1), (1, 0))]
                for i, (c, a, b) in enumerate(terms):
                    ins = pe.matmul(dst, stationary(a, c), moving(b, c), start=i == 0, stop=i == len(terms) - 1)
                return ins

            hT, cT, gT, oT = (hT_hi, hT_lo), (cT_hi, cT_lo), (g_hi, g_lo), (oT_hi, oT_lo)
            wt = (w_hi, w_lo)

            def iteration(n):
                for n, step in steps_of(TENSOR_ORDER, n):
                    kind = step[0]
                    if kind == "T":
                        l = step[1]
                        for s in range(NB):
                            t, tile = gnn_tile("T", l, s)
                            if l == 0:
                                pe.wait_ge(x_normed.sem, x_normed.at(n, s + 1))
                            else:
                                pe.wait_ge(h_next.sem, h_next.at(n, NB * (l - 1) + s + 1))
                            if gnn_free.due(n, gnn_before(t) + 1):
                                pe.wait_ge(gnn_free.sem, gnn_free.at(n, gnn_before(t) + 1))
                            src = x_in if l == 0 else z
                            for c in range(KC):
                                ins = pe.transpose(tile[:, c * P:(c + 1) * P], src[:, s, c * P:(c + 1) * P],
                                                   ident[:, :])
                            ins.then_inc(gnn_full.sem, 1)
                    elif kind == "G":
                        _, l, c = step
                        t, tile = gnn_tile("G", l, c)
                        if c == 0:
                            pe.wait_ge(gnn_free.sem, gnn_free.at(n, gnn_tile("T", l, NB - 1)[0] + 1))
                            if isinstance(n, int) and n == 0:
                                pe.wait_ge(piece_lo, KC * (3 * l + 2))
                        if gnn_free.due(n, gnn_before(t) + 1):
                            pe.wait_ge(gnn_free.sem, gnn_free.at(n, gnn_before(t) + 1))
                        for i, side in enumerate(("left", "right")):
                            ins = product(tile[:, i * NODES:(i + 1) * NODES],
                                          lambda a, k: wt[a][f"{side}{l}"][:, k, c * P:(c + 1) * P],
                                          lambda b, k: hT[b][:, k, :])
                        ins.then_inc(gnn_full.sem, 1)
                    elif kind == "H":
                        _, l, s = step
                        t, tile = gnn_tile("H", l, s)
                        if gnn_free.due(n, gnn_before(t) + 1):
                            pe.wait_ge(gnn_free.sem, gnn_free.at(n, gnn_before(t) + 1))
                        if isinstance(n, int) and n == 0:
                            pe.wait_ge(piece_lo, KC * (3 * l + 3))
                        product(tile[:, 0:H], lambda a, k: hT[a][:, k, node_cols(s)],
                                lambda b, k: wt[b][f"lin{l}"][:, k, :]).then_inc(gnn_full.sem, 1)
                    elif kind == "U":
                        _, l, j = step
                        t, tile = gnn_tile("U", l, j)
                        if j == 0:
                            pe.wait_ge(gnn_free.sem, gnn_free.at(n, gnn_tile("G", l, KC - 1)[0] + 1))
                        if gnn_free.due(n, gnn_before(t) + 1):
                            pe.wait_ge(gnn_free.sem, gnn_free.at(n, gnn_before(t) + 1))
                        first = P if j == 0 else 0
                        product(tile[:, 0:3 * P], lambda a, k: hT[a][:, k, node_cols(j)],
                                lambda b, k: gT[b][:, k, first:first + 3 * P]).then_inc(gnn_full.sem, 1)
                    elif kind == "X":
                        _, l, s = step
                        t, tile = gnn_tile("X", l, s)
                        pe.wait_ge(att_ready.sem, att_ready.at(n, NB * (l + 1)))
                        pe.wait_ge(gnn_free.sem, gnn_free.at(n, gnn_tile("H", l, NB - 1)[0] + 1))
                        if gnn_free.due(n, gnn_before(t) + 1):
                            pe.wait_ge(gnn_free.sem, gnn_free.at(n, gnn_before(t) + 1))
                        for j in range(NB):
                            at = (s if j == 0 else 1 - s) * P
                            ins = pe.matmul(tile[:, 0:H + 1], att[:, j, at:at + P], h_lin[:, j, 0:H + 1],
                                            start=j == 0, stop=j == NB - 1)
                        ins.then_inc(gnn_full.sem, 1)
                    elif kind == "CT":
                        s = step[1]
                        pe.wait_ge(c_normed.sem, c_normed.at(n, s + 1))
                        if proj_free.due(n, PROJ[step]):
                            pe.wait_ge(proj_free.sem, proj_free.at(n, PROJ[step]))
                        for c in range(KC):
                            ins = pe.transpose(proj_bank[:, c * P:(c + 1) * P], c_norm[:, s, c * P:(c + 1) * P],
                                               ident[:, :])
                        ins.then_inc(proj_full.sem, 1)
                    elif kind == "QK":
                        c = step[1]
                        if proj_free.due(n, PROJ[step]):
                            pe.wait_ge(proj_free.sem, proj_free.at(n, PROJ[step]))
                        if c == 0:
                            pe.wait_ge(proj_free.sem, proj_free.at(n, PROJ["CT", NB - 1] + 1))
                            if isinstance(n, int) and n == 1:
                                pe.wait_ge(piece_lo, len(pieces))
                        for i, key in enumerate(("q", "k")):
                            ins = product(proj_bank[:, i * NODES:(i + 1) * NODES],
                                          lambda a, k: wt[a][key][:, k, c * P:(c + 1) * P],
                                          lambda b, k: cT[b][:, k, :])
                        ins.then_inc(proj_full.sem, 1)
                    elif kind == "V":
                        s = step[1]
                        if proj_free.due(n, PROJ[step]):
                            pe.wait_ge(proj_free.sem, proj_free.at(n, PROJ[step]))
                        product(proj_bank[:, 0:H], lambda a, k: cT[a][:, k, s * P:(s + 1) * P],
                                lambda b, k: wt[b]["v"][:, k, :]).then_inc(proj_full.sem, 1)
                    elif kind == "S":
                        k = step[1]
                        c, qb, pr = k // PPC, k % PPC // 2, k % 2
                        if k % PPC == 0:
                            pe.wait_ge(spread[c % 2].sem, spread[c % 2].at(n, SPREAD_DMAS * (1 + (c == 2))))
                        if score_free.due(n, k - 1):
                            pe.wait_ge(score_free.sem, score_free.at(n, k - 1))
                        at = qb * P
                        for i in range(2):
                            g = 2 * pr + i
                            ins = pe.matmul(score_bank[k % 2][:, i * NODES:(i + 1) * NODES],
                                            qk_stack[:, c % 2, g, 0, at:at + P], qk_stack[:, c % 2, g, 1, :],
                                            start=True, stop=True)
                        ins.then_inc(score_full.sem, 1)
                    elif kind == "P":
                        k = step[1]
                        pe.wait_ge(prob_ready.sem, prob_ready.at(n, k + 1))
                        if pT_free.due(n, k):
                            pe.wait_ge(pT_free.sem, pT_free.at(n, k))
                        for b in range(NB):
                            for i in range(2):
                                at = (2 * b + i) * P
                                ins = pe.transpose(pT_bank[:, at:at + P], prob[:, k % PROB_BUFS, i, b * P:(b + 1) * P],
                                                   ident[:, :])
                        ins.then_inc(pT_full.sem, 1)
                    elif kind == "O":
                        c = step[1]
                        pe.wait_ge(pT_free.sem, pT_free.at(n, PPC * (c + 1)))
                        pe.wait_ge(proj_free.sem, proj_free.at(n, PROJ["V", NB - 1] + 1))
                        if out_free.due(n, OUT[step]):
                            pe.wait_ge(out_free.sem, out_free.at(n, OUT[step]))
                        for b in range(NB):
                            for g in range(HPC):
                                head = HPC * c + g
                                ins = pe.matmul(out_bank[g * D:(g + 1) * D, 0:NODES], v[:, b, head * D:(head + 1) * D],
                                          prob_t[:, b, g, :], start=b == 0, stop=b == NB - 1)
                        ins.then_inc(out_full.sem, 1)
                    elif kind == "Y":
                        s = step[1]
                        pe.wait_ge(out_free.sem, out_free.at(n, KC))
                        if out_free.due(n, OUT[step]):
                            pe.wait_ge(out_free.sem, out_free.at(n, OUT[step]))
                        product(out_bank[:, 0:H], lambda a, k: oT[a][:, k, s * P:(s + 1) * P],
                                lambda b, k: wt[b]["o"][:, k, :]).then_inc(out_full.sem, 1)

            pe.wait_ge(consts, 5)
            iteration(0)
            iteration(1)
            iteration(2)
            with pe.Fori(3, GRAPHS - 1) as n:
                iteration(n)
            iteration(GRAPHS - 1)
            iteration(GRAPHS)
            iteration(GRAPHS + 1)


def kernel(**inputs):
    import numpy as np
    import concourse.bacc as bacc
    from concourse.bass_utils import run_bass_kernel_spmd

    a = {k: np.asarray(t) for k, t in inputs.items()}
    adj = a["adj"]
    blocks = adj.transpose(0, 2, 1).reshape(GRAPHS, NB, P, NB, P)
    adj_t = np.stack([blocks[:, 0], blocks[:, 1, :, ::-1]], axis=1).reshape(GRAPHS, NB, P, NODES)
    by_feature = np.arange(H).reshape(KC, HPC, D).transpose(0, 2, 1).reshape(-1)
    w = {
        "q": a["L1_gnn_Wq"].T[:, by_feature], "k": a["L1_gnn_Wk"].T[:, by_feature],
        "v": a["L1_gnn_Wv"].T, "o": a["L1_gnn_Wo"].T,
    }
    for l in range(LAYERS):
        w[f"left{l}"], w[f"right{l}"] = a["L0_gnn_W_left"][l], a["L0_gnn_W_right"][l]
        w[f"lin{l}"] = a["L0_gnn_W_lin"][l].T
    arrays = {
        "in_x": a["x"], "in_adj": adj, "in_adj_t": adj_t, "in_w": np.stack([w[k] for k in WEIGHTS]),
        "in_vec": np.concatenate([a["L0_gnn_b_lin"], a["L0_gnn_ln_a"], a["L0_gnn_ln_b"],
                                  a["L1_gnn_bv"][None], a["L1_gnn_bo"][None]]),
    }
    arrays = {k: np.ascontiguousarray(t) for k, t in arrays.items()}
    nc = bacc.Bacc("TRN2", target_bir_lowering=False, num_devices=1)
    args = [nc.dram_tensor(k, t.shape, mybir.dt.from_np(t.dtype), kind="ExternalInput").ap() for k, t in arrays.items()]
    args.append(nc.dram_tensor("out", (GRAPHS, NODES, H), F32, kind="ExternalOutput").ap())
    build(nc, *args)
    return run_bass_kernel_spmd(nc, [arrays], core_ids=[0]).results[0]["out"]
```
